# Optimizing a Trainium2 kernel written in Bass

```python
import numpy as np
import jax
import jax.numpy as jnp

def _softmax(x, axis=-1):
    return jax.nn.softmax(x, axis=axis)

def _gelu(x):
    return jax.nn.gelu(x, approximate=True)

def _silu(x):
    return jax.nn.silu(x)

def _sigmoid(x):
    return jax.nn.sigmoid(x)

def _layernorm(x, axis=-1, eps=1e-05):
    m = jnp.mean(x, axis=axis, keepdims=True)
    v = jnp.var(x, axis=axis, keepdims=True)
    return (x - m) / jnp.sqrt(v + eps)

def _scatter_add(tgt, idx, src, axis=0):
    return tgt.at[idx].add(src)

def _segment_sum(src, seg, n):
    return jax.ops.segment_sum(src, seg, n)
kernel_name = 'mk_adaln_ffn_d1_seqx_r4_23ee62'

def setup_inputs(seed: int=0):
    np.random.seed(seed)
    _w = jnp.asarray

    def _rec_inputs():
        import jax
        import jax.numpy as jnp
        _rk = jax.random.key(seed)
        x = -0.0003929 + 0.9999 * jax.random.normal(jax.random.fold_in(_rk, 1), (2, 1024, 256), jnp.float32)
        _lenS = 1024 - jax.random.randint(jax.random.fold_in(_rk, 7), (2,), 0, max(1, 1024 // 4) + 1, jnp.int32)
        _lenS2 = 1024 - jax.random.randint(jax.random.fold_in(_rk, 8), (2,), 0, max(1, 1024 // 4) + 1, jnp.int32)
        cond_256 = -0.0209273 + 1.04763 * jax.random.normal(jax.random.fold_in(_rk, 11), (2, 64), jnp.float32)
        return (x, cond_256)
    x, cond_256 = _rec_inputs()

    def _L0_cond_setup():
        import jax, jax.numpy as jnp
        import numpy as np
        EPS = 1e-08

        def hamilton(q1, q2):
            w1, x1, y1, z1 = (q1[..., i, :] for i in range(4))
            w2, x2, y2, z2 = (q2[..., i, :] for i in range(4))
            w = w1 * w2 - x1 * x2 - y1 * y2 - z1 * z2
            x = w1 * x2 + x1 * w2 + y1 * z2 - z1 * y2
            y = w1 * y2 - x1 * z2 + y1 * w2 + z1 * x2
            z = w1 * z2 + x1 * y2 - y1 * x2 + z1 * w2
            return jnp.stack([w, x, y, z], axis=-2)

        def _normalize(q):
            return q / jnp.sqrt(jnp.sum(q * q, axis=0, keepdims=True) + EPS)
        key = jax.random.key(seed)
        k1, k2, k3, k4 = jax.random.split(key, 4)
        B, T, d_model = (4, 1024, 256)
        quat_dim = d_model // 4
        x = jax.random.normal(k1, (B, T, d_model), dtype=jnp.float32)
        q_left = jax.random.normal(k2, (4, quat_dim), dtype=jnp.float32)
        q_right = jax.random.normal(k3, (4, quat_dim), dtype=jnp.float32)
        spectral_gate = jax.random.uniform(k4, (1, 1, 1, quat_dim), dtype=jnp.float32)
        return {'x': x, 'q_left': q_left, 'q_right': q_right, 'spectral_gate': spectral_gate}
    _L0_cond_all = _L0_cond_setup()
    _L0_cond_in = {k: v for k, v in _L0_cond_all.items() if k in ('q_right', 'spectral_gate')}
    del _L0_cond_all

    def _L0_ffn_setup():
        import jax, jax.numpy as jnp
        import numpy as np
        E = 8
        key = jax.random.key(seed)
        k0, k1, k2, k3 = jax.random.split(key, 4)
        B, S, H, F = (4, 1024, 256, 1024)
        x = jax.random.normal(k0, (B, S, H), jnp.float32)
        Wr = jax.random.normal(k1, (E, H), jnp.float32) * 0.02
        W1 = jax.random.normal(k2, (E, H, F), jnp.float32) * 0.02
        b1 = jnp.zeros((E, F), jnp.float32)
        W2 = jax.random.normal(k3, (E, F, H), jnp.float32) * 0.02
        b2 = jnp.zeros((E, H), jnp.float32)
        return {'x': x, 'Wr': Wr, 'W1': W1, 'b1': b1, 'W2': W2, 'b2': b2}
    _L0_ffn_all = _L0_ffn_setup()
    _L0_ffn_in = {k: v for k, v in _L0_ffn_all.items() if k in ('Wr', 'W1', 'b1', 'W2', 'b2')}
    del _L0_ffn_all
    return {'x': x, 'cond_256': cond_256, 'L0_cond_q_right': _L0_cond_in['q_right'], 'L0_cond_spectral_gate': _L0_cond_in['spectral_gate'], 'L0_ffn_Wr': _L0_ffn_in['Wr'], 'L0_ffn_W1': _L0_ffn_in['W1'], 'L0_ffn_b1': _L0_ffn_in['b1'], 'L0_ffn_W2': _L0_ffn_in['W2'], 'L0_ffn_b2': _L0_ffn_in['b2']}

def reference(x, cond_256, L0_cond_q_right, L0_cond_spectral_gate, L0_ffn_Wr, L0_ffn_W1, L0_ffn_b1, L0_ffn_W2, L0_ffn_b2):
    import jax
    import jax.numpy as jnp

    def _L0_cond_ref(x, q_left, q_right, spectral_gate):
        import jax, jax.numpy as jnp
        import numpy as np
        EPS = 1e-08

        def hamilton(q1, q2):
            w1, x1, y1, z1 = (q1[..., i, :] for i in range(4))
            w2, x2, y2, z2 = (q2[..., i, :] for i in range(4))
            w = w1 * w2 - x1 * x2 - y1 * y2 - z1 * z2
            x = w1 * x2 + x1 * w2 + y1 * z2 - z1 * y2
            y = w1 * y2 - x1 * z2 + y1 * w2 + z1 * x2
            z = w1 * z2 + x1 * y2 - y1 * x2 + z1 * w2
            return jnp.stack([w, x, y, z], axis=-2)

        def _normalize(q):
            return q / jnp.sqrt(jnp.sum(q * q, axis=0, keepdims=True) + EPS)
        B, T, d_model = x.shape
        quat_dim = d_model // 4
        x_quat = x.reshape(B, T, 4, quat_dim)
        x_spectral = jnp.fft.fft(x_quat, axis=1)
        x_filtered = jnp.fft.ifft(x_spectral * spectral_gate, axis=1).real.astype(x.dtype)
        q_left_n = _normalize(q_left)
        q_right_n = _normalize(q_right)
        conj_sign = jnp.array([1.0, -1.0, -1.0, -1.0], dtype=x.dtype)[:, None]
        q_right_conj = q_right_n * conj_sign
        x_right = hamilton(x_filtered, q_right_conj)
        x_rotated = hamilton(q_left_n, x_right)
        return x_rotated.reshape(B, T, d_model)

    def _L0_ffn_ref(x, Wr, W1, b1, W2, b2):
        import jax, jax.numpy as jnp
        import numpy as np
        E = 8
        B, S, H = x.shape
        xf = x.reshape(-1, H)
        probs = jax.nn.softmax(xf @ Wr.T, axis=-1)
        eid = E - 1
        h = jax.nn.gelu(xf @ W1[eid] + b1[eid], approximate=False)
        y = (h @ W2[eid] + b2[eid]) * probs[:, eid:eid + 1]
        return y.reshape(B, S, H)
    x = x + _L0_ffn_ref(_L0_cond_ref(x, cond_256, L0_cond_q_right, L0_cond_spectral_gate), L0_ffn_Wr, L0_ffn_W1, L0_ffn_b1, L0_ffn_W2, L0_ffn_b2)
    return x

_drawn_inputs = setup_inputs


def setup_inputs(seed=0):
    import zlib

    import numpy as np

    out = dict(_drawn_inputs(seed))
    spreads = {'L0_ffn_b1': (0.0, 0.8), 'L0_ffn_b2': (0.0, 0.613)}
    factors = {'cond_256': 4.916,
     'L0_cond_q_right': 4.464,
     'L0_cond_spectral_gate': 7.619,
     'L0_ffn_Wr': 8.0,
     'L0_ffn_W1': 4.579,
     'L0_ffn_W2': 4.243}
    for name, (base, spread) in spreads.items():
        noise = np.random.default_rng([zlib.crc32(name.encode()), seed]).standard_normal(out[name].shape)
        drawn = base * np.exp(spread * noise) if base else spread * noise
        out[name] = jnp.asarray(drawn.astype(out[name].dtype))
    for name, factor in factors.items():
        out[name] = (out[name] * factor).astype(out[name].dtype)
    return out
```

```python
from contextlib import ExitStack

import numpy as np

import concourse.bass as bass
from concourse import mybir

F32 = mybir.dt.float32
F32R = mybir.dt.float32r
ALU = mybir.AluOpType
ACT = mybir.ActivationFunctionType
AX = mybir.AxisListType

P = 128
EPS = 1e-8


def lane_selection(n_quat):
    w, x, y, z = 2, 3, 4, 5
    B = [[(w, 1), (x, 1), (y, 1), (z, 1)],
         [(x, -1), (w, 1), (z, -1), (y, 1)],
         [(y, -1), (z, 1), (w, 1), (x, -1)],
         [(z, -1), (y, -1), (x, 1), (w, 1)]]
    J = [[0, -1, -1, -1], [1, 0, -1, 1], [1, 1, 0, -1], [1, -1, 1, 0]]
    sel = np.zeros((14, 16 + 7), np.float32)
    for half in range(2):
        for ko in range(2):
            o = 2 * ko + half
            for c in range(n_quat):
                row, sign = B[o][c]
                sel[7 * half + row, 4 * ko + c] += sign
                for k in range(4):
                    row, sign = B[k][c]
                    sel[7 * half + row, 8 + 4 * ko + c] += J[o][k] * sign
        for r in range(7):
            sel[7 * half + r, 16 + r] = 1
    return sel


def adaln_ffn(nc, x, cond, q_right, gate, Wr, W1, b1, W2, b2, sel, out):
    n_batch, n_seq, C = x.shape
    n_experts, _, F = W1.shape
    E7 = n_experts - 1
    LANES = C // 4
    BLOCK = 512
    N_BLOCKS = n_batch * n_seq // BLOCK
    TT = BLOCK // P
    KC = C // P
    FT = F // P
    SLOTS = 4
    LAG = 2
    TAIL = LAG + 1
    NE = n_experts
    CHUNKS = [(0, NE + 2 * P), (NE + 2 * P, 3 * P), (NE + 5 * P, 3 * P)]
    assert C == 2 * P and CHUNKS[-1][0] + CHUNKS[-1][1] == NE + F and FT % SLOTS == 0

    x_blocks = x.rearrange("a (b p j) c -> (a b) p j c", p=P, j=TT)
    out_blocks = out.rearrange("a (b p j) c -> (a b) p j c", p=P, j=TT)

    with ExitStack() as ctx:
        def sb(name, shape, dt=F32):
            return ctx.enter_context(nc.sbuf_tensor(name, shape, dt))

        def sem(name):
            return ctx.enter_context(nc.semaphore(name))

        ident = sb("ident", [P, P])
        lane_eye = sb("lane_eye", [P, LANES])
        q_rows = sb("q_rows", [14, P])
        sel_sb = sb("sel_sb", [14, 23])
        coef = sb("coef", [P, 23])
        squares = sb("squares", [P, 6])
        norms = sb("norms", [P, 2])
        inv_norms = sb("inv_norms", [P, 2])
        minus_half = sb("minus_half", [P, 2])
        vJB = sb("vJB", [P, 8])
        M_raw = sb("M_raw", [P, 8])
        M_lane = sb("M_lane", [P, 8])
        R = sb("R", [P, 2 * 4, LANES])
        small_rows = sb("small_rows", [FT, C + P])
        w_cat = sb("w_cat", [P, KC, NE + F])
        b1_cols = sb("b1_cols", [P, FT])
        b2_all = sb("b2_all", [P, C])
        w2 = sb("w2", [P, FT, C])
        w1_hi = sb("w1_hi", [P, KC, F], F32R)
        w1_lo = sb("w1_lo", [P, KC, F], F32R)
        wr_hi_lo = sb("wr_hi_lo", [P, KC, 2 * NE], F32R)
        w2_hi = sb("w2_hi", [P, FT, C], F32R)
        w2_lo = sb("w2_lo", [P, FT, C], F32R)
        x_in = sb("x_in", [P, TT, C])
        xT_hi = sb("xT_hi", [P, KC, BLOCK], F32R)
        xT_lo = sb("xT_lo", [P, KC, BLOCK], F32R)
        h_all = sb("h_all", [P, SLOTS, BLOCK])
        h_hi = sb("h_hi", [P, SLOTS, BLOCK], F32R)
        h_lo = sb("h_lo", [P, SLOTS, BLOCK], F32R)
        logitsT = sb("logitsT", [2 * NE, BLOCK])
        logits = sb("logits", [P, TT, NE])
        logit_max = sb("logit_max", [P, TT])
        shifted = sb("shifted", [P, TT, NE])
        e_const = sb("e_const", [P, 1])
        exps = sb("exps", [P, TT, NE])
        exp_sum = sb("exp_sum", [P, TT])
        inv_sum = sb("inv_sum", [P, TT])
        prob = sb("prob", [P, TT])
        prob_b2 = sb("prob_b2", [P, TT, C])
        rest = sb("rest", [P, TT, C])
        y = sb("y", [P, TT, C])

        acc = [ctx.enter_context(nc.psum_tensor(f"acc{i}", [P, 512], F32)) for i in range(2)]
        pre = [ctx.enter_context(nc.psum_tensor(f"pre{i}", [P, 512], F32)) for i in range(2)]
        xT_ps = [ctx.enter_context(nc.psum_tensor(f"xT_ps{i}", [P, 512], F32)) for i in range(2)]
        lT_ps = ctx.enter_context(nc.psum_tensor("lT_ps", [2 * NE, BLOCK], F32))
        small_ps = ctx.enter_context(nc.psum_tensor("small_ps", [P, 512], F32))
        coef_ps = small_ps[:, 0:23]
        wrT_ps = small_ps[:, 32:32 + KC * NE].rearrange("p (k e) -> p k e", k=KC)
        b1_ps = small_ps[:, 64:64 + FT]
        logits_ps = small_ps[:, 128:128 + TT * 2 * NE].rearrange("p (j e) -> p j e", j=TT)
        fold_banks = [acc, pre, acc]

        q_zeroed = sem("q_zeroed")
        q_loaded = sem("q_loaded")
        small_loaded = sem("small_loaded")
        w1_loaded = [sem(f"w1_loaded{i}") for i in range(len(CHUNKS))]
        x_loaded = sem("x_loaded")
        w2_loaded = sem("w2_loaded")
        b2_loaded = sem("b2_loaded")
        stored = sem("stored")
        zeroed = sem("zeroed")
        ident_ready = sem("ident_ready")
        consts_ready = sem("consts_ready")
        inv_norms_ready = sem("inv_norms_ready")
        w2_hi_ready = sem("w2_hi_ready")
        w2_lo_ready = sem("w2_lo_ready")
        coef_done = sem("coef_done")
        small_transposed = sem("small_transposed")
        small_copied = sem("small_copied")
        step = sem("step")
        norms_ready = sem("norms_ready")
        R_ready = sem("R_ready")
        folded = sem("folded")
        fold_hi_ready = sem("fold_hi_ready")
        fold_lo_ready = sem("fold_lo_ready")
        xT_done = sem("xT_done")
        xT_hi_ready = sem("xT_hi_ready")
        xT_lo_ready = sem("xT_lo_ready")
        logitsT_done = sem("logitsT_done")
        logitsT_copied = sem("logitsT_copied")
        logits_done = sem("logits_done")
        logits_summed = sem("logits_summed")
        max_ready = sem("max_ready")
        shifted_ready = sem("shifted_ready")
        exps_ready = sem("exps_ready")
        sum_ready = sem("sum_ready")
        inv_sum_ready = sem("inv_sum_ready")
        prob_ready = sem("prob_ready")
        prob_b2_ready = sem("prob_b2_ready")
        rest_ready = sem("rest_ready")
        pre_done = sem("pre_done")
        h_hi_ready = sem("h_hi_ready")
        h_ready = sem("h_ready")
        h_lo_ready = sem("h_lo_ready")
        acc_done = sem("acc_done")
        y_ready = sem("y_ready")

        block = ctx.enter_context(nc.Block())

        def chunk_cols(i):
            start, n = CHUNKS[i]
            skip = NE if i == 0 else 0
            return start + skip - NE, n - skip, skip

        @block.sync
        def _(sp):
            def load_w1(i):
                at, n, _ = chunk_cols(i)
                sp.dma_start(w_cat[:, :, NE + at:NE + at + n],
                             W1[E7, :, at:at + n].rearrange("(k p) f -> p k f", p=P)).then_inc(w1_loaded[i], 16)

            sp.dma_start(x_in[:, :, :], x_blocks[0]).then_inc(x_loaded, 16)
            for i in range(len(CHUNKS)):
                load_w1(i)
            with sp.Fori(1, N_BLOCKS) as b:
                sp.wait_ge(rest_ready, b)
                sp.dma_start(x_in[:, :, :], x_blocks[b]).then_inc(x_loaded, 16)
                sp.wait_ge(y_ready, TT * b)
                sp.dma_start(out_blocks[b - 1], y[:, :, :]).then_inc(stored, 16)
            sp.wait_ge(y_ready, TT * N_BLOCKS)
            sp.dma_start(out_blocks[N_BLOCKS - 1], y[:, :, :]).then_inc(stored, 16)
            sp.wait_ge(stored, 16 * N_BLOCKS + 1)

        @block.gpsimd
        def _(pool):
            nc.gpsimd.memset(ident[:, :], 0.0).then_inc(zeroed, 1)
            pool.wait_ge(zeroed, 1)
            nc.gpsimd.affine_select(out=ident[:, :], in_=ident[:, :], compare_op=ALU.not_equal, fill=1.0,
                                    base=0, pattern=[[-1, P]], channel_multiplier=1).then_inc(ident_ready, 1)
            pool.wait_ge(ident_ready, 1)
            nc.gpsimd.memset(minus_half[:, :], -0.5).then_inc(consts_ready, 1)
            nc.gpsimd.memset(e_const[:, :], float(np.e)).then_inc(consts_ready, 1)
            nc.gpsimd.tensor_tensor(lane_eye[:, :], ident[:, 0:LANES], ident[:, LANES:2 * LANES],
                                    ALU.add).then_inc(consts_ready, 1)
            pool.wait_ge(consts_ready, 3)
            pool.wait_ge(norms_ready, 1)
            nc.gpsimd.tensor_tensor(inv_norms[:, :], norms[:, :], minus_half[:, :], ALU.pow).then_inc(inv_norms_ready, 1)
            for i in range(2):
                half = slice(i * FT // 2, (i + 1) * FT // 2)
                pool.wait_ge(w2_hi_ready, i + 1)
                nc.gpsimd.tensor_tensor(w2_lo[:, half, :], w2[:, half, :], w2_hi[:, half, :].bitcast(F32),
                                        ALU.subtract).then_inc(w2_lo_ready, 1)

            def softmax_and_rest(b):
                pool.wait_ge(max_ready, b + 1)
                nc.gpsimd.tensor_tensor(shifted[:, :, :], logits[:, :, :],
                                        logit_max[:, :].unsqueeze(2).to_broadcast([P, TT, NE]),
                                        ALU.subtract).then_inc(shifted_ready, 1)
                pool.wait_ge(shifted_ready, b + 1)
                nc.gpsimd.tensor_tensor(exps[:, :, :], e_const[:, :].unsqueeze(2).to_broadcast([P, TT, NE]),
                                        shifted[:, :, :], ALU.pow).then_inc(exps_ready, 1)
                pool.wait_ge(prob_ready, b + 1)
                if isinstance(b, int):
                    pool.wait_ge(b2_loaded, 16)
                nc.gpsimd.tensor_tensor(prob_b2[:, :, :], b2_all[:, :].unsqueeze(1).to_broadcast([P, TT, C]),
                                        prob[:, :].unsqueeze(2).to_broadcast([P, TT, C]),
                                        ALU.mult).then_inc(prob_b2_ready, 1)
                pool.wait_ge(prob_b2_ready, b + 1)
                if not isinstance(b, int):
                    pool.wait_ge(y_ready, TT * b)
                pool.wait_ge(x_loaded, 16 * b + 16)
                nc.gpsimd.tensor_tensor(rest[:, :, :], prob_b2[:, :, :], x_in[:, :, :], ALU.add).then_inc(rest_ready, 1)

            softmax_and_rest(0)
            with pool.Fori(1, N_BLOCKS) as b:
                softmax_and_rest(b)

        @block.scalar
        def _(act):
            act.wait_ge(q_zeroed, 1)
            for half in range(2):
                lanes = slice(half * LANES, (half + 1) * LANES)
                at = 7 * half
                act.dma_start(q_rows[at:at + 2, lanes], cond).then_inc(q_loaded, 16)
                act.dma_start(q_rows[at + 2:at + 6, lanes], q_right).then_inc(q_loaded, 16)
                act.dma_start(q_rows[at + 6:at + 7, lanes], gate[0, 0]).then_inc(q_loaded, 16)
            act.dma_start(sel_sb[:, :], sel).then_inc(q_loaded, 16)
            act.dma_start(small_rows[:, 0:C], Wr).then_inc(small_loaded, 16)
            act.dma_start(small_rows[:, C:C + P], b1[E7].rearrange("(t p) -> t p", p=P)).then_inc(small_loaded, 16)
            act.dma_start(w2[:, :, :], W2[E7].rearrange("(t p) c -> p t c", p=P)).then_inc(w2_loaded, 16)
            act.dma_start(b2_all[:, :], b2[E7:E7 + 1, :].to_broadcast([P, C])).then_inc(b2_loaded, 16)

            def split_x(b):
                for k in range(KC):
                    act.wait_ge(xT_done, KC * b + k + 1)
                    if k == 0 and not isinstance(b, int):
                        act.wait_ge(pre_done, FT * b)
                    nc.scalar.activation(xT_hi[:, k, :], xT_ps[k][:, :], ACT.Copy).then_inc(xT_hi_ready, 1)

            def hidden(b):
                act.wait_ge(logitsT_done, b + 1)
                if not isinstance(b, int):
                    act.wait_ge(logits_done, b)
                nc.scalar.activation(logitsT[:, :], lT_ps[:, :], ACT.Copy).then_inc(logitsT_copied, 1)
                for f in range(FT):
                    act.wait_ge(pre_done, FT * b + f + 1)
                    if not (isinstance(b, int) and f < SLOTS):
                        act.wait_ge(acc_done, FT * b + f + 1 - SLOTS)
                    s = f % SLOTS
                    nc.scalar.activation(h_hi[:, s, :], pre[f % 2][:, :], ACT.Gelu,
                                         bias=b1_cols[:, f:f + 1]).then_inc(h_hi_ready, 1)
                    nc.scalar.activation(h_all[:, s, :], pre[f % 2][:, :], ACT.Gelu,
                                         bias=b1_cols[:, f:f + 1]).then_inc(h_ready, 1)

            split_x(0)
            for i in range(len(CHUNKS)):
                at, n, skip = chunk_cols(i)
                for k in range(KC):
                    act.wait_ge(folded, KC * i + k + 1)
                    if i == 0:
                        nc.scalar.activation(wr_hi_lo[:, k, 0:NE], fold_banks[i][k][:, 0:NE],
                                             ACT.Copy).then_inc(fold_hi_ready, 1)
                    nc.scalar.activation(w1_hi[:, k, at:at + n], fold_banks[i][k][:, skip:skip + n],
                                         ACT.Copy).then_inc(fold_hi_ready, 1)
            act.wait_ge(small_copied, 2)
            hidden(0)
            with act.Fori(1, N_BLOCKS) as b:
                split_x(b)
                hidden(b)

        @block.vector
        def _(dve):
            nc.vector.memset(q_rows[:, :], 0.0).then_inc(q_zeroed, 1)
            nc.vector.memset(y[:, 0, 0:1], 0.0).then_inc(stored, 1)

            dve.wait_ge(small_transposed, 1)
            nc.vector.tensor_copy(w_cat[:, :, 0:NE], wrT_ps).then_inc(small_copied, 1)
            nc.vector.tensor_copy(b1_cols[:, :], b1_ps).then_inc(small_copied, 1)

            chain = [0]

            def link(instruction):
                chain[0] += 1
                instruction.then_inc(step, 1)
                dve.wait_ge(step, chain[0])

            dve.wait_ge(coef_done, 1)
            link(nc.vector.tensor_copy(coef[:, :], coef_ps))
            a, v, g = coef[:, 16:17], coef[:, 17:18], coef[:, 22:23]
            link(nc.vector.tensor_tensor(squares[:, :], coef[:, 16:22], coef[:, 16:22], ALU.mult))
            nc.vector.tensor_reduce(norms[:, 0:1], squares[:, 0:2], AX.X, ALU.add)
            link(nc.vector.tensor_reduce(norms[:, 1:2], squares[:, 2:6], AX.X, ALU.add))
            nc.vector.tensor_scalar(norms[:, :], norms[:, :], EPS, None, ALU.add).then_inc(norms_ready, 1)
            link(nc.vector.tensor_scalar(vJB[:, :], coef[:, 8:16], v, None, ALU.mult))
            link(nc.vector.scalar_tensor_tensor(out=M_raw[:, :], in0=coef[:, 0:8], scalar=a, in1=vJB[:, :],
                                                op0=ALU.mult, op1=ALU.add))
            dve.wait_ge(inv_norms_ready, 1)
            link(nc.vector.tensor_scalar(M_lane[:, :], M_raw[:, :], g, inv_norms[:, 0:1], ALU.mult, ALU.mult))
            dve.wait_ge(consts_ready, 3)
            nc.vector.scalar_tensor_tensor(
                out=R[:, :, :], in0=lane_eye[:, :].unsqueeze(1).to_broadcast([P, 8, LANES]),
                scalar=inv_norms[:, 1:2], in1=M_lane[:, :].unsqueeze(2).to_broadcast([P, 8, LANES]),
                op0=ALU.mult, op1=ALU.mult).then_inc(R_ready, 1)

            def split_x(b):
                for k in range(KC):
                    dve.wait_ge(xT_hi_ready, KC * b + k + 1)
                    nc.vector.tensor_tensor(xT_lo[:, k, :], xT_ps[k][:, :], xT_hi[:, k, :].bitcast(F32),
                                            ALU.subtract).then_inc(xT_lo_ready, 1)

            def finish(b):
                dve.wait_ge(acc_done, FT * b)
                dve.wait_ge(rest_ready, b)
                dve.wait_ge(stored, 16 * (b - 1) + 1)
                for j in range(TT):
                    nc.vector.scalar_tensor_tensor(
                        out=y[:, j, :], in0=acc[j // 2][:, (j % 2) * C:(j % 2 + 1) * C],
                        scalar=prob[:, j:j + 1], in1=rest[:, j, :], op0=ALU.mult, op1=ALU.add).then_inc(y_ready, 1)

            def low_hidden(b, f):
                s = f % SLOTS
                dve.wait_ge(h_ready, FT * b + f + 1)
                nc.vector.tensor_tensor(h_lo[:, s, :], h_all[:, s, :], h_hi[:, s, :].bitcast(F32),
                                        ALU.subtract).then_inc(h_lo_ready, 1)

            def hidden_and_softmax(b):
                low_hidden(b, 0)
                dve.wait_ge(logits_done, b + 1)
                nc.vector.tensor_reduce(logits[:, :, :], logits_ps.rearrange("p j (h e) -> p j e h", h=2),
                                        AX.X, ALU.add).then_inc(logits_summed, 1)
                dve.wait_ge(logits_summed, b + 1)
                nc.vector.tensor_reduce(logit_max[:, :], logits[:, :, :], AX.X, ALU.max).then_inc(max_ready, 1)
                for f in range(1, 5):
                    low_hidden(b, f)
                dve.wait_ge(exps_ready, b + 1)
                nc.vector.tensor_reduce(exp_sum[:, :], exps[:, :, :], AX.X, ALU.add).then_inc(sum_ready, 1)
                dve.wait_ge(sum_ready, b + 1)
                nc.vector.reciprocal(inv_sum[:, :], exp_sum[:, :]).then_inc(inv_sum_ready, 1)
                dve.wait_ge(inv_sum_ready, b + 1)
                nc.vector.tensor_tensor(prob[:, :], exps[:, :, E7], inv_sum[:, :], ALU.mult).then_inc(prob_ready, 1)
                for f in range(5, FT):
                    low_hidden(b, f)

            split_x(0)
            n_hi = 0
            for i in range(len(CHUNKS)):
                at, n, skip = chunk_cols(i)
                for k in range(KC):
                    n_hi += 2 if i == 0 else 1
                    dve.wait_ge(fold_hi_ready, n_hi)
                    if i == 0:
                        nc.vector.tensor_tensor(wr_hi_lo[:, k, NE:2 * NE], fold_banks[i][k][:, 0:NE],
                                                wr_hi_lo[:, k, 0:NE].bitcast(F32), ALU.subtract).then_inc(fold_lo_ready, 1)
                    nc.vector.tensor_tensor(w1_lo[:, k, at:at + n], fold_banks[i][k][:, skip:skip + n],
                                            w1_hi[:, k, at:at + n].bitcast(F32), ALU.subtract).then_inc(fold_lo_ready, 1)
            dve.wait_ge(w2_loaded, 16)
            for i in range(2):
                half = slice(i * FT // 2, (i + 1) * FT // 2)
                nc.vector.tensor_copy(w2_hi[:, half, :], w2[:, half, :]).then_inc(w2_hi_ready, 1)

            hidden_and_softmax(0)
            with dve.Fori(1, N_BLOCKS) as b:
                split_x(b)
                finish(b)
                hidden_and_softmax(b)
            finish(N_BLOCKS)

        @block.tensor
        def _(pe):
            pe.wait_ge(ident_ready, 1)
            pe.wait_ge(small_loaded, 32)
            for k in range(KC):
                nc.tensor.transpose(wrT_ps[:, k, :], small_rows[:, k * P:(k + 1) * P], ident[0:NE, 0:NE])
            nc.tensor.transpose(b1_ps, small_rows[:, C:C + P], ident[0:FT, 0:FT]).then_inc(small_transposed, 1)
            pe.wait_ge(q_loaded, 7 * 16)
            pe.wait_ge(small_copied, 2)
            nc.tensor.matmul(coef_ps, q_rows[:, :], sel_sb[:, :], start=True, stop=True).then_inc(coef_done, 1)

            def transpose_x(b):
                pe.wait_ge(x_loaded, 16 * b + 16)
                for k in range(KC):
                    if not isinstance(b, int):
                        pe.wait_ge(xT_lo_ready, KC * b)
                    for j in range(TT):
                        last = nc.tensor.transpose(xT_ps[k][:, j * P:(j + 1) * P],
                                                   x_in[:, j, k * P:(k + 1) * P], ident[:, :])
                    last.then_inc(xT_done, 1)

            def fold(i):
                start, n = CHUNKS[i]
                pe.wait_ge(w1_loaded[i], 16)
                if i == 2:
                    pe.wait_ge(fold_lo_ready, 2 * KC)
                for kc in range(KC):
                    for ko in range(KC):
                        last = nc.tensor.matmul(fold_banks[i][kc][:, 0:n],
                                                R[:, 4 * ko + 2 * kc:4 * ko + 2 * kc + 2, :],
                                                w_cat[:, ko, start:start + n], start=(ko == 0), stop=(ko == KC - 1))
                    last.then_inc(folded, 1)

            def router(b):
                if isinstance(b, int):
                    pe.wait_ge(fold_lo_ready, 2 * KC)
                else:
                    pe.wait_ge(logitsT_copied, b)
                for k in range(KC):
                    pe.wait_ge(xT_hi_ready, KC * b + k + 1)
                    nc.tensor.matmul(lT_ps[:, :], wr_hi_lo[:, k, :], xT_hi[:, k, :], start=(k == 0), stop=False)
                for k in range(KC):
                    pe.wait_ge(xT_lo_ready, KC * b + k + 1)
                    last = nc.tensor.matmul(lT_ps[:, :], wr_hi_lo[:, k, :], xT_lo[:, k, :], start=False,
                                            stop=(k == KC - 1))
                last.then_inc(logitsT_done, 1)

            def wait_for_logits(b):
                pe.wait_ge(logitsT_copied, b + 1)
                if not isinstance(b, int):
                    pe.wait_ge(logits_summed, b)

            def transpose_logits(b):
                for j in range(TT):
                    last = nc.tensor.transpose(logits_ps[:, j, :], logitsT[:, j * P:(j + 1) * P],
                                               ident[0:2 * NE, 0:2 * NE])
                last.then_inc(logits_done, 1)

            def first_product(b, f):
                bank = pre[f % 2]
                cols = slice(f * P, (f + 1) * P)
                if not (isinstance(b, int) and f < 2):
                    pe.wait_ge(h_ready, FT * b + f - 1)
                for n, (w, xT) in enumerate(((w1_hi, xT_hi), (w1_hi, xT_lo), (w1_lo, xT_hi))):
                    for k in range(KC):
                        last = nc.tensor.matmul(bank[:, :], w[:, k, cols], xT[:, k, :],
                                                start=(n == 0 and k == 0), stop=(n == 2 and k == KC - 1))
                last.then_inc(pre_done, 1)

            def second_product(b, f):
                s = f % SLOTS
                if f == 0 and not isinstance(b, int):
                    pe.wait_ge(y_ready, TT * b)
                pe.wait_ge(h_hi_ready, FT * b + f + 1)
                for j in range(TT):
                    half = acc[j // 2][:, (j % 2) * C:(j % 2 + 1) * C]
                    for n, w in enumerate((w2_hi, w2_lo)):
                        nc.tensor.matmul(half, h_hi[:, s, j * P:(j + 1) * P], w[:, f, :],
                                         start=(f == 0 and j % 2 == 0 and n == 0), stop=False, skip_group_check=True)
                pe.wait_ge(h_lo_ready, FT * b + f + 1)
                for j in range(TT):
                    half = acc[j // 2][:, (j % 2) * C:(j % 2 + 1) * C]
                    last = nc.tensor.matmul(half, h_lo[:, s, j * P:(j + 1) * P], w2_hi[:, f, :], start=False,
                                            stop=(f == FT - 1), skip_group_check=True)
                last.then_inc(acc_done, 1)

            def products(b):
                for f in range(FT):
                    if f == 1:
                        wait_for_logits(b)
                    first_product(b, f)
                    if f == 1:
                        transpose_logits(b)
                    if f >= LAG and f - LAG < FT - TAIL:
                        if isinstance(b, int) and f == LAG:
                            pe.wait_ge(w2_lo_ready, 2)
                        second_product(b, f - LAG)

            transpose_x(0)
            pe.wait_ge(R_ready, 1)
            pe.wait_ge(small_copied, 1)
            for i in range(len(CHUNKS)):
                fold(i)
            router(0)
            pe.wait_ge(fold_lo_ready, KC * (len(CHUNKS) + 1))
            products(0)
            with pe.Fori(1, N_BLOCKS) as b:
                transpose_x(b)
                for f in range(FT - TAIL, FT):
                    second_product(b - 1, f)
                router(b)
                products(b)
            for f in range(FT - TAIL, FT):
                second_product(N_BLOCKS - 1, f)


_INS = ["x", "cond_256", "L0_cond_q_right", "L0_cond_spectral_gate", "L0_ffn_Wr", "L0_ffn_W1", "L0_ffn_b1",
        "L0_ffn_W2", "L0_ffn_b2"]


def kernel(**inputs):
    import concourse.bacc as _bacc
    from concourse.bass_utils import run_bass_kernel_spmd as _run

    nc = _bacc.Bacc("TRN2", target_bir_lowering=False, num_devices=1)
    arrays, args = {}, []
    for name in _INS:
        arrays[f"in_{name}"] = np.ascontiguousarray(inputs[name])
    arrays["lane_selection"] = lane_selection(4)
    for name, a in arrays.items():
        args.append(nc.dram_tensor(name, a.shape, mybir.dt.from_np(a.dtype), kind="ExternalInput").ap())
    out = nc.dram_tensor("out", inputs["x"].shape, F32, kind="ExternalOutput").ap()
    adaln_ffn(nc, *args, out)
    r = _run(nc, [arrays], core_ids=[0])
    return r.results[0]["out"]
```

```python
from contextlib import ExitStack

import numpy as np

import concourse.bass as bass
from concourse import mybir

F32 = mybir.dt.float32
F32R = mybir.dt.float32r
ALU = mybir.AluOpType
ACT = mybir.ActivationFunctionType
AX = mybir.AxisListType

P = 128
EPS = 1e-8


def lane_selection(n_quat):
    w, x, y, z = 2, 3, 4, 5
    B = [[(w, 1), (x, 1), (y, 1), (z, 1)],
         [(x, -1), (w, 1), (z, -1), (y, 1)],
         [(y, -1), (z, 1), (w, 1), (x, -1)],
         [(z, -1), (y, -1), (x, 1), (w, 1)]]
    J = [[0, -1, -1, -1], [1, 0, -1, 1], [1, 1, 0, -1], [1, -1, 1, 0]]
    sel = np.zeros((7, 2, 16 + 7), np.float32)
    for half in range(2):
        for ko in range(2):
            o = 2 * ko + half
            for c in range(n_quat):
                row, sign = B[o][c]
                sel[row, half, 4 * ko + c] += sign
                for k in range(4):
                    row, sign = B[k][c]
                    sel[row, half, 8 + 4 * ko + c] += J[o][k] * sign
        for r in range(7):
            sel[r, half, 16 + r] = 1
    return sel.reshape(7, 2 * 23)


def adaln_ffn(nc, x, quat_rows, router_rows, W1, W2, b2, out):
    n_batch, n_seq, C = x.shape
    n_experts, _, F = W1.shape
    E7 = n_experts - 1
    LANES = C // 4
    BLOCK = 512
    N_BLOCKS = n_batch * n_seq // BLOCK
    TT = BLOCK // P
    KC = C // P
    FT = F // P
    SLOTS = 4
    LAG = 2
    TAIL = LAG + 1
    NE = n_experts
    N_SEL = 23
    WARM_UP_MORE = 2
    WARM_UP = 5
    CHUNKS = [(0, NE + 2 * P), (NE + 2 * P, 3 * P), (NE + 5 * P, 3 * P)]
    assert C == 2 * P and CHUNKS[-1][0] + CHUNKS[-1][1] == NE + F and FT % SLOTS == 0

    x_blocks = x.rearrange("a (b p j) c -> (a b) p j c", p=P, j=TT)
    out_blocks = out.rearrange("a (b p j) c -> (a b) p j c", p=P, j=TT)

    with ExitStack() as ctx:
        def sb(name, shape, dt=F32):
            return ctx.enter_context(nc.sbuf_tensor(name, shape, dt))

        def sem(name):
            return ctx.enter_context(nc.semaphore(name))

        ident = sb("ident", [P, P])
        lane_eye = sb("lane_eye", [P, LANES])
        quats = sb("quats", [7, LANES + 2 * N_SEL])
        coef = sb("coef", [P, 23])
        squares = sb("squares", [P, 6])
        norms = sb("norms", [P, 2])
        inv_norms = sb("inv_norms", [P, 2])
        minus_half = sb("minus_half", [P, 2])
        vJB = sb("vJB", [P, 8])
        M_raw = sb("M_raw", [P, 8])
        M_lane = sb("M_lane", [P, 8])
        M_hi = sb("M_hi", [P, 8], F32R)
        M_lo = sb("M_lo", [P, 8], F32R)
        R_hi = sb("R_hi", [P, 2 * 4, LANES], F32R)
        R_lo = sb("R_lo", [P, 2 * 4, LANES], F32R)
        w_cat_hi = sb("w_cat_hi", [P, KC, NE + F], F32R)
        w_cat_lo = sb("w_cat_lo", [P, KC, NE + F], F32R)
        small_rows = sb("small_rows", [FT, C + P])
        w_cat = sb("w_cat", [P, KC, NE + F])
        b1_cols = sb("b1_cols", [P, FT])
        b2_all = sb("b2_all", [P, C])
        w2 = sb("w2", [P, FT, C])
        w1_hi = sb("w1_hi", [P, KC, F], F32R)
        w1_lo = sb("w1_lo", [P, KC, F], F32R)
        wr_hi_lo = sb("wr_hi_lo", [P, KC, 2 * NE], F32R)
        w2_hi = sb("w2_hi", [P, FT, C], F32R)
        w2_lo = sb("w2_lo", [P, FT, C], F32R)
        x_in = sb("x_in", [P, TT, C])
        x_keep = sb("x_keep", [P, TT, C])
        xT_hi = sb("xT_hi", [P, KC, BLOCK], F32R)
        xT_lo = sb("xT_lo", [P, KC, BLOCK], F32R)
        h_all = sb("h_all", [P, SLOTS, BLOCK])
        h_hi = sb("h_hi", [P, SLOTS, BLOCK], F32R)
        h_lo = sb("h_lo", [P, SLOTS, BLOCK], F32R)
        logitsT = sb("logitsT", [2 * NE, BLOCK])
        logits = sb("logits", [P, TT, NE])
        logit_max = sb("logit_max", [P, TT])
        shifted = sb("shifted", [P, TT, NE])
        e_const = sb("e_const", [P, 1])
        exps = sb("exps", [P, TT, NE])
        exp_sum = sb("exp_sum", [P, TT])
        inv_sum = sb("inv_sum", [P, TT])
        prob = sb("prob", [P, TT])
        prob_b2 = sb("prob_b2", [P, TT, C])
        rest = sb("rest", [P, TT, C])
        y = sb("y", [P, TT, C])
        warm = sb("warm", [P, 1])

        acc = [ctx.enter_context(nc.psum_tensor(f"acc{i}", [P, 512], F32)) for i in range(2)]
        pre = [ctx.enter_context(nc.psum_tensor(f"pre{i}", [P, 512], F32)) for i in range(2)]
        xT_ps = [ctx.enter_context(nc.psum_tensor(f"xT_ps{i}", [P, 512], F32)) for i in range(2)]
        lT_bank = ctx.enter_context(nc.psum_tensor("lT_bank", [P, 512], F32))
        lT_ps = lT_bank[0:2 * NE, :]
        lT_warm = lT_bank[:, 0:P]
        small_ps = ctx.enter_context(nc.psum_tensor("small_ps", [P, 512], F32))
        coef_ps = pre[0][:, 0:N_SEL]
        wrT_ps = small_ps[:, 32:32 + KC * NE].rearrange("p (k e) -> p k e", k=KC)
        b1_ps = small_ps[:, 64:64 + FT]
        logits_ps = small_ps[:, 128:128 + TT * 2 * NE].rearrange("p (j e) -> p j e", j=TT)
        fold_banks = [acc, pre, acc]

        q_loaded = sem("q_loaded")
        small_loaded = sem("small_loaded")
        w1_loaded = [sem(f"w1_loaded{i}") for i in range(len(CHUNKS))]
        x_loaded = sem("x_loaded")
        w2_loaded = sem("w2_loaded")
        b2_loaded = sem("b2_loaded")
        stored = sem("stored")
        warm_zeroed = sem("warm_zeroed")
        zeroed = sem("zeroed")
        ident_ready = sem("ident_ready")
        consts_ready = sem("consts_ready")
        inv_norms_ready = sem("inv_norms_ready")
        w2_hi_ready = sem("w2_hi_ready")
        w2_lo_ready = sem("w2_lo_ready")
        coef_done = sem("coef_done")
        small_transposed = sem("small_transposed")
        small_copied = sem("small_copied")
        step = sem("step")
        norms_ready = sem("norms_ready")
        M_lo_ready = sem("M_lo_ready")
        R_hi_ready = sem("R_hi_ready")
        R_lo_ready = sem("R_lo_ready")
        w_cat_hi_ready = sem("w_cat_hi_ready")
        w_cat_lo_ready = sem("w_cat_lo_ready")
        folded = sem("folded")
        fold_hi_ready = sem("fold_hi_ready")
        fold_lo_ready = sem("fold_lo_ready")
        xT_done = sem("xT_done")
        x_kept = sem("x_kept")
        xT_hi_ready = sem("xT_hi_ready")
        xT_lo_ready = sem("xT_lo_ready")
        logitsT_done = sem("logitsT_done")
        logitsT_copied = sem("logitsT_copied")
        logits_done = sem("logits_done")
        logits_summed = sem("logits_summed")
        max_ready = sem("max_ready")
        shifted_ready = sem("shifted_ready")
        exps_ready = sem("exps_ready")
        sum_ready = sem("sum_ready")
        inv_sum_ready = sem("inv_sum_ready")
        prob_ready = sem("prob_ready")
        prob_b2_ready = sem("prob_b2_ready")
        rest_ready = sem("rest_ready")
        pre_done = sem("pre_done")
        h_hi_ready = sem("h_hi_ready")
        h_ready = sem("h_ready")
        h_lo_ready = sem("h_lo_ready")
        acc_done = sem("acc_done")
        bank_done = sem("bank_done")
        y_ready = sem("y_ready")

        block = ctx.enter_context(nc.Block())

        def chunk_cols(i):
            start, n = CHUNKS[i]
            skip = NE if i == 0 else 0
            return start + skip - NE, n - skip, skip

        @block.sync
        def _(sp):
            def load_w1(i):
                at, n, _ = chunk_cols(i)
                sp.dma_start(w_cat[:, :, NE + at:NE + at + n],
                             W1[E7, :, at:at + n].rearrange("(k p) f -> p k f", p=P)).then_inc(w1_loaded[i], 16)

            sp.dma_start(quats[:, :], quat_rows).then_inc(q_loaded, 16)
            load_w1(0)
            sp.dma_start(x_in[:, :, :], x_blocks[0]).then_inc(x_loaded, 16)
            load_w1(1)
            load_w1(2)
            sp.dma_start(w2[:, :, :], W2[E7].rearrange("(t p) c -> p t c", p=P)).then_inc(w2_loaded, 16)
            with sp.Fori(1, N_BLOCKS) as b:
                sp.wait_ge(x_kept, b)
                sp.dma_start(x_in[:, :, :], x_blocks[b]).then_inc(x_loaded, 16)
                sp.wait_ge(y_ready, TT * b)
                sp.dma_start(out_blocks[b - 1], y[:, :, :]).then_inc(stored, 16)
            sp.wait_ge(y_ready, TT * (N_BLOCKS - 1) + 2)
            sp.dma_start(out_blocks[N_BLOCKS - 1, :, 0:2, :], y[:, 0:2, :]).then_inc(stored, 16)
            sp.wait_ge(y_ready, TT * N_BLOCKS)
            sp.dma_start(out_blocks[N_BLOCKS - 1, :, 3:4, :], y[:, 3:4, :]).then_inc(stored, 16)
            sp.wait_ge(stored, 16 * (N_BLOCKS + 2) + 1)

        @block.gpsimd
        def _(pool):
            nc.gpsimd.memset(ident[:, :], 0.0).then_inc(zeroed, 1)
            pool.wait_ge(zeroed, 1)
            nc.gpsimd.affine_select(out=ident[:, :], in_=ident[:, :], compare_op=ALU.not_equal, fill=1.0,
                                    base=0, pattern=[[-1, P]], channel_multiplier=1).then_inc(ident_ready, 1)
            pool.wait_ge(ident_ready, 1)
            nc.gpsimd.memset(minus_half[:, :], -0.5).then_inc(consts_ready, 1)
            nc.gpsimd.memset(e_const[:, :], float(np.e)).then_inc(consts_ready, 1)
            nc.gpsimd.tensor_tensor(lane_eye[:, :], ident[:, 0:LANES], ident[:, LANES:2 * LANES],
                                    ALU.add).then_inc(consts_ready, 1)
            pool.dma_start(b2_all[:, :], b2[E7:E7 + 1, :].to_broadcast([P, C])).then_inc(b2_loaded, 16)
            pool.wait_ge(consts_ready, 3)
            pool.wait_ge(norms_ready, 1)
            nc.gpsimd.tensor_tensor(inv_norms[:, :], norms[:, :], minus_half[:, :], ALU.pow).then_inc(inv_norms_ready, 1)
            pool.wait_ge(M_lo_ready, 1)
            nc.gpsimd.tensor_tensor(R_lo[:, :, :], lane_eye[:, :].unsqueeze(1).to_broadcast([P, 8, LANES]),
                                    M_lo[:, :].bitcast(F32).unsqueeze(2).to_broadcast([P, 8, LANES]),
                                    ALU.mult).then_inc(R_lo_ready, 1)
            for i in range(2):
                half = slice(i * FT // 2, (i + 1) * FT // 2)
                pool.wait_ge(w2_hi_ready, i + 1)
                nc.gpsimd.tensor_tensor(w2_lo[:, half, :], w2[:, half, :], w2_hi[:, half, :].bitcast(F32),
                                        ALU.subtract).then_inc(w2_lo_ready, 1)

            def softmax_and_rest(b):
                pool.wait_ge(max_ready, b + 1)
                nc.gpsimd.tensor_tensor(shifted[:, :, :], logits[:, :, :],
                                        logit_max[:, :].unsqueeze(2).to_broadcast([P, TT, NE]),
                                        ALU.subtract).then_inc(shifted_ready, 1)
                pool.wait_ge(shifted_ready, b + 1)
                nc.gpsimd.tensor_tensor(exps[:, :, :], e_const[:, :].unsqueeze(2).to_broadcast([P, TT, NE]),
                                        shifted[:, :, :], ALU.pow).then_inc(exps_ready, 1)
                pool.wait_ge(prob_ready, b + 1)
                nc.gpsimd.tensor_tensor(prob_b2[:, :, :], b2_all[:, :].unsqueeze(1).to_broadcast([P, TT, C]),
                                        prob[:, :].unsqueeze(2).to_broadcast([P, TT, C]),
                                        ALU.mult).then_inc(prob_b2_ready, 1)
                pool.wait_ge(prob_b2_ready, b + 1)
                if not isinstance(b, int):
                    pool.wait_ge(y_ready, TT * b)
                pool.wait_ge(x_kept, b + 1)
                nc.gpsimd.tensor_tensor(rest[:, :, :], prob_b2[:, :, :], x_keep[:, :, :], ALU.add).then_inc(rest_ready, 1)

            pool.wait_ge(b2_loaded, 16)
            softmax_and_rest(0)
            with pool.Fori(1, N_BLOCKS) as b:
                softmax_and_rest(b)

        @block.scalar
        def _(act):
            act.dma_start(small_rows[:, :], router_rows).then_inc(small_loaded, 16)

            act.wait_ge(warm_zeroed, 1)
            nc.scalar.activation(warm[:, :], warm[:, :], ACT.Gelu)

            def split_x(b):
                for k in range(KC):
                    act.wait_ge(xT_done, KC * b + k + 1)
                    if k == 0 and not isinstance(b, int):
                        act.wait_ge(pre_done, FT * b)
                    nc.scalar.activation(xT_hi[:, k, :], xT_ps[k][:, :], ACT.Copy).then_inc(xT_hi_ready, 1)

            def hidden(b):
                act.wait_ge(logitsT_done, b + 1)
                if not isinstance(b, int):
                    act.wait_ge(logits_done, b)
                nc.scalar.activation(logitsT[:, :], lT_ps, ACT.Copy).then_inc(logitsT_copied, 1)
                for f in range(FT):
                    act.wait_ge(pre_done, FT * b + f + 1)
                    if not (isinstance(b, int) and f < SLOTS):
                        if f == SLOTS - 1:
                            act.wait_ge(bank_done, 2 * b)
                        elif f < SLOTS - 1:
                            act.wait_ge(acc_done, (FT - 1) * (b - 1) + FT + f + 1 - SLOTS)
                        else:
                            act.wait_ge(acc_done, (FT - 1) * b + f + 1 - SLOTS)
                    s = f % SLOTS
                    nc.scalar.activation(h_hi[:, s, :], pre[f % 2][:, :], ACT.Gelu,
                                         bias=b1_cols[:, f:f + 1]).then_inc(h_hi_ready, 1)
                    nc.scalar.activation(h_all[:, s, :], pre[f % 2][:, :], ACT.Gelu,
                                         bias=b1_cols[:, f:f + 1]).then_inc(h_ready, 1)

            def split_w_cat(i):
                start, n = CHUNKS[i]
                act.wait_ge(w1_loaded[i], 16)
                if i == 0:
                    act.wait_ge(small_copied, 1)
                nc.scalar.activation(w_cat_hi[:, :, start:start + n], w_cat[:, :, start:start + n],
                                     ACT.Copy).then_inc(w_cat_hi_ready, 1)

            split_w_cat(0)
            split_x(0)
            split_w_cat(1)
            split_w_cat(2)
            for i in range(len(CHUNKS)):
                at, n, skip = chunk_cols(i)
                for k in range(KC):
                    act.wait_ge(folded, KC * i + k + 1)
                    if i == 0:
                        nc.scalar.activation(wr_hi_lo[:, k, 0:NE], fold_banks[i][k][:, 0:NE],
                                             ACT.Copy).then_inc(fold_hi_ready, 1)
                    nc.scalar.activation(w1_hi[:, k, at:at + n], fold_banks[i][k][:, skip:skip + n],
                                         ACT.Copy).then_inc(fold_hi_ready, 1)
            act.wait_ge(small_copied, 2)
            hidden(0)
            with act.Fori(1, N_BLOCKS) as b:
                split_x(b)
                hidden(b)
            act.wait_ge(y_ready, TT * N_BLOCKS - 1)
            act.dma_start(out_blocks[N_BLOCKS - 1, :, 2:3, :], y[:, 2:3, :]).then_inc(stored, 16)

        @block.vector
        def _(dve):
            nc.vector.memset(y[:, 0, 0:1], 0.0).then_inc(stored, 1)
            nc.vector.memset(warm[:, :], 0.0).then_inc(warm_zeroed, 1)

            chain = [0]

            def link(instruction):
                chain[0] += 1
                instruction.then_inc(step, 1)
                dve.wait_ge(step, chain[0])

            dve.wait_ge(coef_done, 1)
            link(nc.vector.tensor_copy(coef[:, :], coef_ps))
            a, v, g = coef[:, 16:17], coef[:, 17:18], coef[:, 22:23]
            link(nc.vector.tensor_tensor(squares[:, :], coef[:, 16:22], coef[:, 16:22], ALU.mult))
            nc.vector.tensor_reduce(norms[:, 0:1], squares[:, 0:2], AX.X, ALU.add)
            link(nc.vector.tensor_reduce(norms[:, 1:2], squares[:, 2:6], AX.X, ALU.add))
            nc.vector.tensor_scalar(norms[:, :], norms[:, :], EPS, None, ALU.add).then_inc(norms_ready, 1)
            link(nc.vector.tensor_scalar(vJB[:, :], coef[:, 8:16], v, None, ALU.mult))
            link(nc.vector.scalar_tensor_tensor(out=M_raw[:, :], in0=coef[:, 0:8], scalar=a, in1=vJB[:, :],
                                                op0=ALU.mult, op1=ALU.add))
            dve.wait_ge(small_transposed, 1)
            nc.vector.tensor_copy(w_cat[:, :, 0:NE], wrT_ps).then_inc(small_copied, 1)
            nc.vector.tensor_copy(b1_cols[:, :], b1_ps).then_inc(small_copied, 1)
            dve.wait_ge(inv_norms_ready, 1)
            link(nc.vector.tensor_scalar(vJB[:, :], M_raw[:, :], g, inv_norms[:, 0:1], ALU.mult, ALU.mult))
            link(nc.vector.tensor_scalar(M_lane[:, :], vJB[:, :], inv_norms[:, 1:2], None, ALU.mult))
            link(nc.vector.tensor_copy(M_hi[:, :], M_lane[:, :]))
            nc.vector.tensor_tensor(M_lo[:, :], M_lane[:, :], M_hi[:, :].bitcast(F32), ALU.subtract).then_inc(M_lo_ready, 1)
            dve.wait_ge(consts_ready, 3)
            nc.vector.tensor_tensor(R_hi[:, :, :], lane_eye[:, :].unsqueeze(1).to_broadcast([P, 8, LANES]),
                                    M_hi[:, :].bitcast(F32).unsqueeze(2).to_broadcast([P, 8, LANES]),
                                    ALU.mult).then_inc(R_hi_ready, 1)

            def split_w_cat(i):
                start, n = CHUNKS[i]
                dve.wait_ge(w_cat_hi_ready, i + 1)
                nc.vector.tensor_tensor(w_cat_lo[:, :, start:start + n], w_cat[:, :, start:start + n],
                                        w_cat_hi[:, :, start:start + n].bitcast(F32),
                                        ALU.subtract).then_inc(w_cat_lo_ready, 1)

            def split_x(b):
                for k in range(KC):
                    dve.wait_ge(xT_hi_ready, KC * b + k + 1)
                    nc.vector.tensor_tensor(xT_lo[:, k, :], xT_ps[k][:, :], xT_hi[:, k, :].bitcast(F32),
                                            ALU.subtract).then_inc(xT_lo_ready, 1)

            def finish(b):
                dve.wait_ge(rest_ready, b)
                dve.wait_ge(stored, 16 * (b - 1) + 1)
                for j in range(TT):
                    if j % 2 == 0:
                        dve.wait_ge(bank_done, 2 * (b - 1) + j // 2 + 1)
                    nc.vector.scalar_tensor_tensor(
                        out=y[:, j, :], in0=acc[j // 2][:, (j % 2) * C:(j % 2 + 1) * C],
                        scalar=prob[:, j:j + 1], in1=rest[:, j, :], op0=ALU.mult, op1=ALU.add).then_inc(y_ready, 1)

            def low_hidden(b, f):
                s = f % SLOTS
                dve.wait_ge(h_ready, FT * b + f + 1)
                nc.vector.tensor_tensor(h_lo[:, s, :], h_all[:, s, :], h_hi[:, s, :].bitcast(F32),
                                        ALU.subtract).then_inc(h_lo_ready, 1)

            def hidden_and_softmax(b):
                low_hidden(b, 0)
                dve.wait_ge(logits_done, b + 1)
                nc.vector.tensor_reduce(logits[:, :, :], logits_ps.rearrange("p j (h e) -> p j e h", h=2),
                                        AX.X, ALU.add).then_inc(logits_summed, 1)
                dve.wait_ge(logits_summed, b + 1)
                nc.vector.tensor_reduce(logit_max[:, :], logits[:, :, :], AX.X, ALU.max).then_inc(max_ready, 1)
                low_hidden(b, 1)
                if not isinstance(b, int):
                    dve.wait_ge(rest_ready, b)
                else:
                    dve.wait_ge(x_loaded, 16)
                nc.vector.tensor_copy(x_keep[:, :, :], x_in[:, :, :]).then_inc(x_kept, 1)
                for f in range(2, 5):
                    low_hidden(b, f)
                dve.wait_ge(exps_ready, b + 1)
                nc.vector.tensor_reduce(exp_sum[:, :], exps[:, :, :], AX.X, ALU.add).then_inc(sum_ready, 1)
                dve.wait_ge(sum_ready, b + 1)
                nc.vector.reciprocal(inv_sum[:, :], exp_sum[:, :]).then_inc(inv_sum_ready, 1)
                dve.wait_ge(inv_sum_ready, b + 1)
                nc.vector.tensor_tensor(prob[:, :], exps[:, :, E7], inv_sum[:, :], ALU.mult).then_inc(prob_ready, 1)
                for f in range(5, FT):
                    low_hidden(b, f)

            split_w_cat(0)
            split_x(0)
            n_hi = 0
            for i in range(len(CHUNKS)):
                if i + 1 < len(CHUNKS):
                    split_w_cat(i + 1)
                if i == len(CHUNKS) - 1:
                    dve.wait_ge(w2_loaded, 16)
                    for half in (slice(0, FT // 2), slice(FT // 2, FT)):
                        nc.vector.tensor_copy(w2_hi[:, half, :], w2[:, half, :]).then_inc(w2_hi_ready, 1)
                at, n, skip = chunk_cols(i)
                for k in range(KC):
                    n_hi += 2 if i == 0 else 1
                    dve.wait_ge(fold_hi_ready, n_hi)
                    if i == 0:
                        nc.vector.tensor_tensor(wr_hi_lo[:, k, NE:2 * NE], fold_banks[i][k][:, 0:NE],
                                                wr_hi_lo[:, k, 0:NE].bitcast(F32), ALU.subtract).then_inc(fold_lo_ready, 1)
                    nc.vector.tensor_tensor(w1_lo[:, k, at:at + n], fold_banks[i][k][:, skip:skip + n],
                                            w1_hi[:, k, at:at + n].bitcast(F32), ALU.subtract).then_inc(fold_lo_ready, 1)
            hidden_and_softmax(0)
            with dve.Fori(1, N_BLOCKS) as b:
                split_x(b)
                finish(b)
                hidden_and_softmax(b)
            finish(N_BLOCKS)

        @block.tensor
        def _(pe):
            pe.wait_ge(ident_ready, 1)
            for _ in range(WARM_UP):
                nc.tensor.matmul(lT_warm, ident[:, :], ident[:, :], start=True, stop=True)
            pe.wait_ge(q_loaded, 16)
            for half in range(2):
                rows = slice(half * LANES, (half + 1) * LANES)
                last = nc.tensor.matmul(coef_ps[rows, :], quats[:, 0:LANES],
                                        quats[:, LANES + half * N_SEL:LANES + (half + 1) * N_SEL],
                                        start=True, stop=True)
            last.then_inc(coef_done, 1)
            pe.wait_ge(small_loaded, 16)
            for k in range(KC):
                nc.tensor.transpose(wrT_ps[:, k, :], small_rows[:, k * P:(k + 1) * P], ident[0:NE, 0:NE])
            nc.tensor.transpose(b1_ps, small_rows[:, C:C + P], ident[0:FT, 0:FT]).then_inc(small_transposed, 1)
            for _ in range(WARM_UP_MORE):
                nc.tensor.matmul(lT_warm, ident[:, :], ident[:, :], start=True, stop=True)

            def transpose_x(b):
                pe.wait_ge(x_loaded, 16 * b + 16)
                for k in range(KC):
                    if not isinstance(b, int):
                        pe.wait_ge(xT_lo_ready, KC * b)
                    for j in range(TT):
                        last = nc.tensor.transpose(xT_ps[k][:, j * P:(j + 1) * P],
                                                   x_in[:, j, k * P:(k + 1) * P], ident[:, :])
                    last.then_inc(xT_done, 1)

            def fold(i):
                start, n = CHUNKS[i]
                cols = slice(start, start + n)
                if i == 2:
                    pe.wait_ge(fold_lo_ready, 2 * KC)
                for kc in range(KC):
                    bank = fold_banks[i][kc][:, 0:n]
                    blocks = [slice(4 * ko + 2 * kc, 4 * ko + 2 * kc + 2) for ko in range(KC)]
                    pe.wait_ge(w_cat_hi_ready, i + 1)
                    for ko in range(KC):
                        nc.tensor.matmul(bank, R_hi[:, blocks[ko], :], w_cat_hi[:, ko, cols], start=(ko == 0), stop=False)
                    pe.wait_ge(w_cat_lo_ready, i + 1)
                    for ko in range(KC):
                        nc.tensor.matmul(bank, R_hi[:, blocks[ko], :], w_cat_lo[:, ko, cols], start=False, stop=False)
                    pe.wait_ge(R_lo_ready, 1)
                    for ko in range(KC):
                        last = nc.tensor.matmul(bank, R_lo[:, blocks[ko], :], w_cat_hi[:, ko, cols],
                                                start=False, stop=(ko == KC - 1))
                    last.then_inc(folded, 1)

            def router(b):
                if isinstance(b, int):
                    pe.wait_ge(fold_lo_ready, 2 * KC)
                else:
                    pe.wait_ge(logitsT_copied, b)
                for k in range(KC):
                    pe.wait_ge(xT_hi_ready, KC * b + k + 1)
                    nc.tensor.matmul(lT_ps, wr_hi_lo[:, k, :], xT_hi[:, k, :], start=(k == 0), stop=False)
                for k in range(KC):
                    pe.wait_ge(xT_lo_ready, KC * b + k + 1)
                    last = nc.tensor.matmul(lT_ps, wr_hi_lo[:, k, :], xT_lo[:, k, :], start=False,
                                            stop=(k == KC - 1))
                last.then_inc(logitsT_done, 1)

            def wait_for_logits(b):
                pe.wait_ge(logitsT_copied, b + 1)
                if not isinstance(b, int):
                    pe.wait_ge(logits_summed, b)

            def transpose_logits(b):
                for j in range(TT):
                    last = nc.tensor.transpose(logits_ps[:, j, :], logitsT[:, j * P:(j + 1) * P],
                                               ident[0:2 * NE, 0:2 * NE])
                last.then_inc(logits_done, 1)

            def first_product(b, f):
                if isinstance(b, int) and f in (0, 5):
                    pe.wait_ge(fold_lo_ready, KC * (3 if f == 0 else 4))
                bank = pre[f % 2]
                cols = slice(f * P, (f + 1) * P)
                if not (isinstance(b, int) and f < 2):
                    pe.wait_ge(h_ready, FT * b + f - 1)
                for n, (w, xT) in enumerate(((w1_hi, xT_hi), (w1_hi, xT_lo), (w1_lo, xT_hi))):
                    for k in range(KC):
                        last = nc.tensor.matmul(bank[:, :], w[:, k, cols], xT[:, k, :],
                                                start=(n == 0 and k == 0), stop=(n == 2 and k == KC - 1))
                last.then_inc(pre_done, 1)

            def high(f, bank):
                for j in (2 * bank, 2 * bank + 1):
                    for n, w in enumerate((w2_hi, w2_lo)):
                        nc.tensor.matmul(acc[bank][:, (j % 2) * C:(j % 2 + 1) * C],
                                         h_hi[:, f % SLOTS, j * P:(j + 1) * P], w[:, f, :],
                                         start=(f == 0 and j % 2 == 0 and n == 0), stop=False, skip_group_check=True)

            def low(f, bank):
                for j in (2 * bank, 2 * bank + 1):
                    last = nc.tensor.matmul(acc[bank][:, (j % 2) * C:(j % 2 + 1) * C],
                                            h_lo[:, f % SLOTS, j * P:(j + 1) * P], w2_hi[:, f, :], start=False,
                                            stop=(f == FT - 1), skip_group_check=True)
                return last

            def second_product(b, f):
                if f == 0 and not isinstance(b, int):
                    pe.wait_ge(y_ready, TT * b)
                pe.wait_ge(h_hi_ready, FT * b + f + 1)
                if f == FT - 1:
                    pe.wait_ge(h_lo_ready, FT * b + f + 1)
                    high(f, 0)
                    low(f, 0).then_inc(bank_done, 1)
                    high(f, 1)
                    low(f, 1).then_inc(bank_done, 1)
                    return
                high(f, 0)
                high(f, 1)
                pe.wait_ge(h_lo_ready, FT * b + f + 1)
                low(f, 0)
                low(f, 1).then_inc(acc_done, 1)

            def products(b):
                for f in range(FT):
                    if f == 1:
                        wait_for_logits(b)
                    first_product(b, f)
                    if f == 1:
                        transpose_logits(b)
                    if f >= LAG and f - LAG < FT - TAIL:
                        if isinstance(b, int) and f == LAG:
                            pe.wait_ge(w2_lo_ready, 2)
                            pe.wait_ge(fold_lo_ready, KC * 4)
                        second_product(b, f - LAG)

            transpose_x(0)
            pe.wait_ge(R_hi_ready, 1)
            for i in range(len(CHUNKS)):
                fold(i)
            router(0)
            products(0)
            with pe.Fori(1, N_BLOCKS) as b:
                transpose_x(b)
                for f in range(FT - TAIL, FT):
                    second_product(b - 1, f)
                router(b)
                products(b)
            for f in range(FT - TAIL, FT):
                second_product(N_BLOCKS - 1, f)


def kernel(**inputs):
    import concourse.bacc as _bacc
    from concourse.bass_utils import run_bass_kernel_spmd as _run

    q_right = np.asarray(inputs["L0_cond_q_right"])
    lanes = q_right.shape[1]
    n_experts, hidden = inputs["L0_ffn_b1"].shape
    quat_rows = np.concatenate([inputs["cond_256"], q_right,
                                np.reshape(inputs["L0_cond_spectral_gate"], (1, lanes))], axis=0)
    arrays = {
        "x": inputs["x"],
        "quat_rows": np.concatenate([quat_rows, lane_selection(4)], axis=1),
        "router_rows": np.concatenate([inputs["L0_ffn_Wr"],
                                       np.reshape(inputs["L0_ffn_b1"][n_experts - 1], (hidden // P, P))], axis=1),
        "W1": inputs["L0_ffn_W1"],
        "W2": inputs["L0_ffn_W2"],
        "b2": inputs["L0_ffn_b2"],
    }
    arrays = {name: np.ascontiguousarray(a) for name, a in arrays.items()}
    nc = _bacc.Bacc("TRN2", target_bir_lowering=False, num_devices=1)
    args = [nc.dram_tensor(f"in_{name}", a.shape, mybir.dt.from_np(a.dtype), kind="ExternalInput").ap()
            for name, a in arrays.items()]
    out = nc.dram_tensor("out", arrays["x"].shape, F32, kind="ExternalOutput").ap()
    adaln_ffn(nc, *args, out)
    r = _run(nc, [{f"in_{name}": a for name, a in arrays.items()}], core_ids=[0])
    return r.results[0]["out"]
```

```python
from contextlib import ExitStack

import numpy as np

import concourse.bass as bass
from concourse import mybir

F32 = mybir.dt.float32
F32R = mybir.dt.float32r
ALU = mybir.AluOpType
ACT = mybir.ActivationFunctionType
AX = mybir.AxisListType

P = 128
EPS = 1e-8


def rotation_terms():
    w, x, y, z = range(4)
    B = [[(w, 1), (x, 1), (y, 1), (z, 1)],
         [(x, -1), (w, 1), (z, -1), (y, 1)],
         [(y, -1), (z, 1), (w, 1), (x, -1)],
         [(z, -1), (y, -1), (x, 1), (w, 1)]]
    J = [[0, -1, -1, -1], [1, 0, -1, 1], [1, 1, 0, -1], [1, -1, 1, 0]]
    component = np.zeros((4, 4, 4), int)
    sign = np.zeros((4, 4, 4), np.float32)
    for o in range(4):
        for c in range(4):
            terms = [B[o][c]] + [(B[k][c][0], J[o][k] * B[k][c][1]) for k in range(4) if k != o]
            for t, (q, s) in enumerate(terms):
                component[o, c, t], sign[o, c, t] = q, s
    return component, sign


def adaln_ffn(nc, x, quat_rows, router_rows, W1, W2, b2, out):
    n_batch, n_seq, C = x.shape
    n_experts, _, F = W1.shape
    E7 = n_experts - 1
    LANES = C // 4
    BLOCK = 512
    N_BLOCKS = n_batch * n_seq // BLOCK
    TT = BLOCK // P
    SQ = 32
    QUADS = P // SQ
    KC = C // P
    FT = F // P
    SLOTS = 4
    LAG = 2
    TAIL = LAG + 1
    NE = n_experts
    N_QUAT = 4 + 16 + 1
    WARM_UP = 5
    CHUNKS = [(0, 2 * P), (2 * P, NE + 3 * P), (NE + 5 * P, 3 * P)]
    WR_CHUNK = 1
    WR_AT = CHUNKS[WR_CHUNK][0]
    assert C == KC * P == 2 * P and CHUNKS[-1][0] + CHUNKS[-1][1] == NE + F and FT % SLOTS == 0

    x_blocks = x.rearrange("a (b t s j) c -> (a b) s t j c", t=SQ, s=QUADS, j=TT)
    x_squares = x.rearrange("a (b t n) (q c) -> (a b) q t n c", t=SQ, n=QUADS * TT, q=QUADS)
    out_blocks = out.rearrange("a (b t s j) c -> (a b) s t j c", t=SQ, s=QUADS, j=TT)

    with ExitStack() as ctx:
        def sb(name, shape, dt=F32):
            return ctx.enter_context(nc.sbuf_tensor(name, shape, dt))

        def sem(name):
            return ctx.enter_context(nc.semaphore(name))

        ident = sb("ident", [P, P])
        lane_eye = sb("lane_eye", [P, SQ])
        quats = sb("quats", [P, KC * N_QUAT + 16])
        lane_quats = quats[:, 0:KC * N_QUAT].rearrange("p (k n) -> p k n", k=KC)
        left_terms = lane_quats[:, :, 0:4]
        right_terms = lane_quats[:, :, 4:20]
        gate = lane_quats[:, :, 20:21]
        signs = quats[:, KC * N_QUAT:]
        squares = sb("squares", [P, KC, 2 + 1 + 4 + 1])
        norms = sb("norms", [P, 2, KC])
        inv_norms = sb("inv_norms", [P, 2, KC])
        minus_half = sb("minus_half", [P, 2, KC])
        signed = sb("signed", [P, KC, 16])
        terms = sb("terms", [P, KC * 4, 4])
        M = sb("M", [P, KC * 4])
        gate_left = sb("gate_left", [P, KC])
        lane_scale = sb("lane_scale", [P, KC])
        R = sb("R", [P, KC * 4, SQ])
        small_rows = sb("small_rows", [FT, C + P])
        w_cat = sb("w_cat", [P, KC, NE + F])
        b1_cols = sb("b1_cols", [P, FT])
        b2_all = sb("b2_all", [P, C])
        w2 = sb("w2", [P, FT, C])
        w1_hi = sb("w1_hi", [P, KC, F], F32R)
        w1_lo = sb("w1_lo", [P, KC, F], F32R)
        wr_hi_lo = sb("wr_hi_lo", [P, KC, QUADS, SQ], F32R)
        w2_hi = sb("w2_hi", [P, FT, C], F32R)
        w2_lo = sb("w2_lo", [P, FT, C], F32R)
        x_in = sb("x_in", [P, TT, C])
        x_sq = sb("x_sq", [P, QUADS * TT, LANES])
        xT = sb("xT", [P, KC, BLOCK])
        xT_hi = sb("xT_hi", [P, KC, BLOCK], F32R)
        xT_lo = sb("xT_lo", [P, KC, BLOCK], F32R)
        h_all = sb("h_all", [P, SLOTS, BLOCK])
        h_hi = sb("h_hi", [P, SLOTS, BLOCK], F32R)
        h_lo = sb("h_lo", [P, SLOTS, BLOCK], F32R)
        logits_hi_lo = sb("logits_hi_lo", [P, TT, SQ])
        logits = sb("logits", [P, TT, NE])
        logit_max = sb("logit_max", [P, TT])
        shifted = sb("shifted", [P, TT, NE])
        e_const = sb("e_const", [P, 1])
        exps = sb("exps", [P, TT, NE])
        exp_sum = sb("exp_sum", [P, TT])
        inv_sum = sb("inv_sum", [P, TT])
        prob = sb("prob", [P, TT])
        prob_b2 = sb("prob_b2", [P, TT, C])
        rest = sb("rest", [P, TT, C])
        y = sb("y", [P, TT, C])
        warm = sb("warm", [P, 1])

        acc_banks = [ctx.enter_context(nc.psum_tensor(f"acc{j}", [P, 512], F32)) for j in range(TT)]
        acc = [bank[:, 0:C] for bank in acc_banks]
        pre = [ctx.enter_context(nc.psum_tensor(f"pre{i}", [P, 512], F32)) for i in range(2)]
        xT_ps = acc_banks[2:]
        lT_bank = ctx.enter_context(nc.psum_tensor("lT_bank", [P, 512], F32))
        logitsT = lT_bank[:, :].rearrange("p (j s t) -> p j s t", j=TT, s=QUADS)
        small_ps = ctx.enter_context(nc.psum_tensor("small_ps", [P, 512], F32))
        wrT_ps = small_ps[:, 32:32 + KC * NE].rearrange("p (k e) -> p k e", k=KC)
        b1_ps = small_ps[:, 64:64 + FT]
        fold_banks = [acc_banks[0:2], pre, acc_banks[2:4]]

        q_loaded = sem("q_loaded")
        small_loaded = sem("small_loaded")
        w1_loaded = [sem(f"w1_loaded{i}") for i in range(len(CHUNKS))]
        first_x_loaded = [sem(f"first_x_loaded{i}") for i in range(2)]
        x_loaded = sem("x_loaded")
        x_sq_loaded = sem("x_sq_loaded")
        w2_loaded = [sem(f"w2_loaded{i}") for i in range(2)]
        b2_loaded = sem("b2_loaded")
        stored = sem("stored")
        warm_zeroed = sem("warm_zeroed")
        zeroed = sem("zeroed")
        ident_ready = sem("ident_ready")
        consts_ready = sem("consts_ready")
        inv_norms_ready = sem("inv_norms_ready")
        wr_padded = sem("wr_padded")
        w2_hi_ready = sem("w2_hi_ready")
        w2_lo_ready = sem("w2_lo_ready")
        small_transposed = sem("small_transposed")
        small_copied = sem("small_copied")
        step = sem("step")
        norms_ready = sem("norms_ready")
        R_ready = sem("R_ready")
        scale_ready = sem("scale_ready")
        folded = sem("folded")
        wr_lo_ready = sem("wr_lo_ready")
        fold_hi_ready = sem("fold_hi_ready")
        fold_lo_ready = sem("fold_lo_ready")
        xT_done = sem("xT_done")
        xT_hi_ready = sem("xT_hi_ready")
        xT_lo_ready = sem("xT_lo_ready")
        logitsT_done = sem("logitsT_done")
        logits_turned = sem("logits_turned")
        logits_summed = sem("logits_summed")
        max_ready = sem("max_ready")
        shifted_ready = sem("shifted_ready")
        exps_ready = sem("exps_ready")
        sum_ready = sem("sum_ready")
        inv_sum_ready = sem("inv_sum_ready")
        prob_ready = sem("prob_ready")
        prob_b2_ready = sem("prob_b2_ready")
        rest_ready = sem("rest_ready")
        pre_done = sem("pre_done")
        h_hi_ready = sem("h_hi_ready")
        h_ready = sem("h_ready")
        h_lo_ready = sem("h_lo_ready")
        acc_done = sem("acc_done")
        tile_done = sem("tile_done")
        y_ready = sem("y_ready")

        block = ctx.enter_context(nc.Block())

        def chunk_cols(i):
            start, n = CHUNKS[i]
            skip = NE if i == WR_CHUNK else 0
            return start - (NE if i > WR_CHUNK else 0), n - skip, skip

        def transposed(b, k):
            return xT_ps[k][:, :] if isinstance(b, int) else xT[:, k, :]

        @block.sync
        def _(sp):
            def load_w1(i):
                at, n, skip = chunk_cols(i)
                start = CHUNKS[i][0] + skip
                sp.dma_start(w_cat[:, :, start:start + n],
                             W1[E7, :, at:at + n].rearrange("(p k) f -> p k f", p=P)).then_inc(w1_loaded[i], 16)

            for i in range(2):
                tiles = slice(i * TT // 2, (i + 1) * TT // 2)
                sp.dma_start(x_in[:, tiles, :], x_blocks[0, :, :, tiles, :]).then_inc(first_x_loaded[i], 16)
                if i == 0:
                    sp.dma_start(quats[:, :], quat_rows).then_inc(q_loaded, 16)
            load_w1(0)
            sp.dma_start(small_rows[:, :], router_rows).then_inc(small_loaded, 16)
            load_w1(1)
            load_w1(2)
            w2_tiles = W2[E7].rearrange("(t p) c -> p t c", p=P)
            for i in range(2):
                half = slice(i * FT // 2, (i + 1) * FT // 2)
                sp.dma_start(w2[:, half, :], w2_tiles[:, half, :]).then_inc(w2_loaded[i], 16)
            with sp.Fori(1, N_BLOCKS) as b:
                sp.wait_ge(xT_done, KC * b)
                for q in range(QUADS):
                    sp.dma_start(x_sq[q * SQ:(q + 1) * SQ, :, :], x_squares[b, q]).then_inc(x_sq_loaded, 16)
                sp.wait_ge(rest_ready, b)
                sp.dma_start(x_in[:, :, :], x_blocks[b]).then_inc(x_loaded, 16)
                sp.wait_ge(y_ready, TT * b)
                sp.dma_start(out_blocks[b - 1], y[:, :, :]).then_inc(stored, 16)
            for i in range(2):
                tiles = slice(i * TT // 2, (i + 1) * TT // 2)
                sp.wait_ge(y_ready, TT * (N_BLOCKS - 1) + (i + 1) * TT // 2)
                sp.dma_start(out_blocks[N_BLOCKS - 1, :, :, tiles, :], y[:, tiles, :]).then_inc(stored, 16)
            sp.wait_ge(stored, 16 * (N_BLOCKS + 1) + 1)

        @block.gpsimd
        def _(pool):
            nc.gpsimd.memset(ident[:, :], 0.0).then_inc(zeroed, 1)
            pool.wait_ge(zeroed, 1)
            nc.gpsimd.affine_select(out=ident[:, :], in_=ident[:, :], compare_op=ALU.not_equal, fill=1.0,
                                    base=0, pattern=[[-1, P]], channel_multiplier=1).then_inc(ident_ready, 1)
            pool.wait_ge(ident_ready, 1)
            nc.gpsimd.memset(wr_hi_lo[:, :, :, :].bitcast(F32), 0.0).then_inc(wr_padded, 1)
            nc.gpsimd.memset(minus_half[:, :, :], -0.5).then_inc(consts_ready, 1)
            nc.gpsimd.memset(e_const[:, :], float(np.e)).then_inc(consts_ready, 1)
            pool.wait_ge(consts_ready, 2)
            pool.wait_ge(norms_ready, 2)
            nc.gpsimd.tensor_tensor(inv_norms[:, :, :], norms[:, :, :], minus_half[:, :, :],
                                    ALU.pow).then_inc(inv_norms_ready, 1)
            pool.dma_start(b2_all[:, :], b2[E7:E7 + 1, :].to_broadcast([P, C])).then_inc(b2_loaded, 16)
            for i in range(2):
                half = slice(i * FT // 2, (i + 1) * FT // 2)
                pool.wait_ge(w2_hi_ready, i + 1)
                nc.gpsimd.tensor_tensor(w2_lo[:, half, :], w2[:, half, :], w2_hi[:, half, :].bitcast(F32),
                                        ALU.subtract).then_inc(w2_lo_ready, 1)

            def softmax_and_rest(b):
                pool.wait_ge(max_ready, b + 1)
                nc.gpsimd.tensor_tensor(shifted[:, :, :], logits[:, :, :],
                                        logit_max[:, :].unsqueeze(2).to_broadcast([P, TT, NE]),
                                        ALU.subtract).then_inc(shifted_ready, 1)
                pool.wait_ge(shifted_ready, b + 1)
                nc.gpsimd.tensor_tensor(exps[:, :, :], e_const[:, :].unsqueeze(2).to_broadcast([P, TT, NE]),
                                        shifted[:, :, :], ALU.pow).then_inc(exps_ready, 1)
                pool.wait_ge(prob_ready, b + 1)
                nc.gpsimd.tensor_tensor(prob_b2[:, :, :], b2_all[:, :].unsqueeze(1).to_broadcast([P, TT, C]),
                                        prob[:, :].unsqueeze(2).to_broadcast([P, TT, C]),
                                        ALU.mult).then_inc(prob_b2_ready, 1)
                pool.wait_ge(prob_b2_ready, b + 1)
                if not isinstance(b, int):
                    pool.wait_ge(y_ready, TT * b)
                if isinstance(b, int):
                    pool.wait_ge(first_x_loaded[0], 16)
                    pool.wait_ge(first_x_loaded[1], 16)
                else:
                    pool.wait_ge(x_loaded, 16 * b)
                nc.gpsimd.tensor_tensor(rest[:, :, :], prob_b2[:, :, :], x_in[:, :, :], ALU.add).then_inc(rest_ready, 1)

            pool.wait_ge(b2_loaded, 16)
            softmax_and_rest(0)
            with pool.Fori(1, N_BLOCKS) as b:
                softmax_and_rest(b)

        @block.scalar
        def _(act):
            act.wait_ge(warm_zeroed, 1)
            nc.scalar.activation(warm[:, :], warm[:, :], ACT.Gelu)

            def split_x(b):
                for k in range(KC):
                    act.wait_ge(xT_done, KC * b + k + 1)
                    if k == 0 and not isinstance(b, int):
                        act.wait_ge(pre_done, FT * b)
                    nc.scalar.activation(xT_hi[:, k, :], transposed(b, k), ACT.Copy).then_inc(xT_hi_ready, 1)

            def gelu(b, f):
                act.wait_ge(pre_done, FT * b + f + 1)
                if not (isinstance(b, int) and f < SLOTS):
                    if f == SLOTS - 1:
                        act.wait_ge(tile_done, TT * b)
                    elif f < SLOTS - 1:
                        act.wait_ge(acc_done, (FT - 1) * (b - 1) + FT + f + 1 - SLOTS)
                    else:
                        act.wait_ge(acc_done, (FT - 1) * b + f + 1 - SLOTS)
                s = f % SLOTS
                nc.scalar.activation(h_hi[:, s, :], pre[f % 2][:, :], ACT.Gelu,
                                     bias=b1_cols[:, f:f + 1]).then_inc(h_hi_ready, 1)
                nc.scalar.activation(h_all[:, s, :], pre[f % 2][:, :], ACT.Gelu,
                                     bias=b1_cols[:, f:f + 1]).then_inc(h_ready, 1)

            def hidden(b):
                for f in range(FT - 1):
                    gelu(b, f)

            def split_folded(i):
                at, n, skip = chunk_cols(i)
                for k in range(KC):
                    act.wait_ge(folded, KC * i + k + 1)
                    scale = lane_scale[:, k:k + 1]
                    if i == WR_CHUNK:
                        act.wait_ge(wr_padded, 1)
                        nc.scalar.activation(wr_hi_lo[:, k, :, 0:NE],
                                             fold_banks[i][k][:, 0:NE].unsqueeze(1).to_broadcast([P, QUADS, NE]),
                                             ACT.Copy, scale=scale)
                    nc.scalar.activation(w1_hi[:, k, at:at + n], fold_banks[i][k][:, skip:skip + n],
                                         ACT.Copy, scale=scale).then_inc(fold_hi_ready, 1)

            split_x(0)
            act.wait_ge(scale_ready, 1)
            split_folded(0)
            split_folded(1)
            split_folded(2)
            act.wait_ge(small_copied, 2)
            hidden(0)
            with act.Fori(1, N_BLOCKS) as b:
                split_x(b)
                gelu(b - 1, FT - 1)
                hidden(b)
            gelu(N_BLOCKS - 1, FT - 1)

        @block.vector
        def _(dve):
            nc.vector.memset(y[:, 0, 0:1], 0.0).then_inc(stored, 1)
            nc.vector.memset(warm[:, :], 0.0).then_inc(warm_zeroed, 1)
            nc.vector.memset(squares[:, :, :], EPS).then_inc(step, 1)

            chain = [1]

            def link(instruction):
                chain[0] += 1
                instruction.then_inc(step, 1)
                dve.wait_ge(step, chain[0])

            dve.wait_ge(ident_ready, 1)
            link(nc.vector.tensor_reduce(lane_eye[:, :], ident[:, :].rearrange("p (o l) -> p l o", l=SQ), AX.X, ALU.add))
            dve.wait_ge(q_loaded, 16)
            nc.vector.tensor_tensor(signed[:, :, :], right_terms, signs.unsqueeze(1).to_broadcast([P, KC, 16]),
                                    ALU.mult).then_inc(step, 1)
            nc.vector.tensor_tensor(squares[:, :, 0:2], left_terms[:, :, 0:2], left_terms[:, :, 0:2],
                                    ALU.mult).then_inc(step, 1)
            nc.vector.tensor_tensor(squares[:, :, 3:7], right_terms[:, :, ::4], right_terms[:, :, ::4],
                                    ALU.mult).then_inc(step, 1)
            chain[0] += 3
            dve.wait_ge(step, chain[0])
            for k in range(KC):
                nc.vector.tensor_tensor(terms[:, 4 * k:4 * k + 4, :], signed[:, k, :].rearrange("p (c t) -> p c t", t=4),
                                        left_terms[:, k, :].unsqueeze(1).to_broadcast([P, 4, 4]),
                                        ALU.mult).then_inc(step, 1)
            nc.vector.tensor_reduce(norms[:, 0, :], squares[:, :, 0:3], AX.X, ALU.add).then_inc(norms_ready, 1)
            nc.vector.tensor_reduce(norms[:, 1, :], squares[:, :, 3:8], AX.X, ALU.add).then_inc(norms_ready, 1)
            chain[0] += 2
            dve.wait_ge(step, chain[0])
            link(nc.vector.tensor_reduce(M[:, :], terms[:, :, :], AX.X, ALU.add))
            nc.vector.tensor_tensor(R[:, :, :], lane_eye[:, :].unsqueeze(1).to_broadcast([P, KC * 4, SQ]),
                                    M[:, :].unsqueeze(2).to_broadcast([P, KC * 4, SQ]),
                                    ALU.mult).then_inc(R_ready, 1)
            dve.wait_ge(inv_norms_ready, 1)
            link(nc.vector.tensor_tensor(gate_left[:, :], gate.squeeze(2), inv_norms[:, 0, :], ALU.mult))
            nc.vector.tensor_tensor(lane_scale[:, :], gate_left[:, :], inv_norms[:, 1, :], ALU.mult).then_inc(scale_ready, 1)

            def split_x(b, k):
                dve.wait_ge(xT_hi_ready, KC * b + k + 1)
                nc.vector.tensor_tensor(xT_lo[:, k, :], transposed(b, k), xT_hi[:, k, :].bitcast(F32),
                                        ALU.subtract).then_inc(xT_lo_ready, 1)

            def transpose_x(b):
                dve.wait_ge(x_sq_loaded, 16 * QUADS * b)
                for k in range(KC):
                    nc.vector.transpose(xT[:, k, :].rearrange("p (j s t) -> p j s t", j=TT, s=QUADS),
                                        x_sq[:, :, k::KC].rearrange("p (s j) c -> p j s c", j=TT)
                                        ).then_inc(xT_done, 1)

            def finish(b):
                dve.wait_ge(rest_ready, b)
                dve.wait_ge(stored, 16 * (b - 1) + 1)
                for j in range(TT):
                    dve.wait_ge(tile_done, TT * (b - 1) + j + 1)
                    nc.vector.scalar_tensor_tensor(
                        out=y[:, j, :], in0=acc[j],
                        scalar=prob[:, j:j + 1], in1=rest[:, j, :], op0=ALU.mult, op1=ALU.add).then_inc(y_ready, 1)

            def low_hidden(b, f):
                s = f % SLOTS
                dve.wait_ge(h_ready, FT * b + f + 1)
                nc.vector.tensor_tensor(h_lo[:, s, :], h_all[:, s, :], h_hi[:, s, :].bitcast(F32),
                                        ALU.subtract).then_inc(h_lo_ready, 1)

            def hidden_and_softmax(b):
                low_hidden(b, 0)
                dve.wait_ge(logitsT_done, b + 1)
                for s in range(QUADS):
                    rows = slice(s * SQ, (s + 1) * SQ)
                    nc.vector.transpose(logits_hi_lo[rows, :, :], logitsT[rows, :, s, :]).then_inc(logits_turned, 1)
                dve.wait_ge(logits_turned, QUADS * b + QUADS)
                nc.vector.tensor_reduce(logits[:, :, :],
                                        logits_hi_lo[:, :, 0:2 * NE].rearrange("p j (h e) -> p j e h", h=2),
                                        AX.X, ALU.add).then_inc(logits_summed, 1)
                dve.wait_ge(logits_summed, b + 1)
                nc.vector.tensor_reduce(logit_max[:, :], logits[:, :, :], AX.X, ALU.max).then_inc(max_ready, 1)
                for f in range(1, 5):
                    low_hidden(b, f)
                dve.wait_ge(exps_ready, b + 1)
                nc.vector.tensor_reduce(exp_sum[:, :], exps[:, :, :], AX.X, ALU.add).then_inc(sum_ready, 1)
                dve.wait_ge(sum_ready, b + 1)
                nc.vector.reciprocal(inv_sum[:, :], exp_sum[:, :]).then_inc(inv_sum_ready, 1)
                dve.wait_ge(inv_sum_ready, b + 1)
                nc.vector.tensor_tensor(prob[:, :], exps[:, :, E7], inv_sum[:, :], ALU.mult).then_inc(prob_ready, 1)
                for f in range(5, FT - 1):
                    low_hidden(b, f)

            def split_folded(i):
                at, n, skip = chunk_cols(i)
                for k in range(KC):
                    dve.wait_ge(fold_hi_ready, KC * i + k + 1)
                    scale = lane_scale[:, k:k + 1]
                    if i == WR_CHUNK:
                        nc.vector.scalar_tensor_tensor(
                            out=wr_hi_lo[:, k, :, NE:2 * NE],
                            in0=fold_banks[i][k][:, 0:NE].unsqueeze(1).to_broadcast([P, QUADS, NE]), scalar=scale,
                            in1=wr_hi_lo[:, k, :, 0:NE].bitcast(F32), op0=ALU.mult, op1=ALU.subtract).then_inc(wr_lo_ready, 1)
                    nc.vector.scalar_tensor_tensor(
                        out=w1_lo[:, k, at:at + n], in0=fold_banks[i][k][:, skip:skip + n], scalar=scale,
                        in1=w1_hi[:, k, at:at + n].bitcast(F32), op0=ALU.mult, op1=ALU.subtract).then_inc(fold_lo_ready, 1)

            split_x(0, 0)
            dve.wait_ge(small_transposed, 1)
            nc.vector.tensor_copy(w_cat[:, :, WR_AT:WR_AT + NE], wrT_ps).then_inc(small_copied, 1)
            nc.vector.tensor_copy(b1_cols[:, :], b1_ps).then_inc(small_copied, 1)
            for k in range(1, KC):
                split_x(0, k)
            dve.wait_ge(scale_ready, 1)
            split_folded(0)
            split_folded(1)
            split_folded(2)

            def split_w2(i):
                half = slice(i * FT // 2, (i + 1) * FT // 2)
                dve.wait_ge(w2_loaded[i], 16)
                nc.vector.tensor_copy(w2_hi[:, half, :], w2[:, half, :]).then_inc(w2_hi_ready, 1)

            split_w2(0)
            split_w2(1)

            hidden_and_softmax(0)
            with dve.Fori(1, N_BLOCKS) as b:
                transpose_x(b)
                for k in range(KC):
                    split_x(b, k)
                low_hidden(b - 1, FT - 1)
                finish(b)
                hidden_and_softmax(b)
            low_hidden(N_BLOCKS - 1, FT - 1)
            finish(N_BLOCKS)

        @block.tensor
        def _(pe):
            pe.wait_ge(ident_ready, 1)
            for _ in range(WARM_UP):
                nc.tensor.matmul(lT_bank[:, 0:P], ident[:, :], ident[:, :], start=True, stop=True)

            def transpose_small_rows():
                pe.wait_ge(small_loaded, 16)
                for k in range(KC):
                    nc.tensor.transpose(wrT_ps[:, k, :], small_rows[:, k:C:KC], ident[0:NE, 0:NE])
                nc.tensor.transpose(b1_ps, small_rows[:, C:C + P], ident[0:FT, 0:FT]).then_inc(small_transposed, 1)

            def transpose_first_x():
                channels = x_in[:, :, :].rearrange("p j (m k) -> p j k m", k=KC)
                for i in range(2):
                    pe.wait_ge(first_x_loaded[i], 16)
                    for k in range(KC):
                        for j in range(i * TT // 2, (i + 1) * TT // 2):
                            last = nc.tensor.transpose(xT_ps[k][:, j * P:(j + 1) * P], channels[:, j, k], ident[:, :])
                        if i == 1:
                            last.then_inc(xT_done, 1)

            def fold(i):
                start, n = CHUNKS[i]
                cols = slice(start, start + n)
                if i == 2:
                    pe.wait_ge(xT_lo_ready, KC)
                pe.wait_ge(w1_loaded[i], 16)
                if i == WR_CHUNK:
                    pe.wait_ge(small_copied, 1)
                if i == 0:
                    pe.wait_ge(R_ready, 1)
                for k in range(KC):
                    if i == 0 and k == 1:
                        transpose_small_rows()
                    nc.tensor.matmul(fold_banks[i][k][:, 0:n], R[:, 4 * k:4 * k + 4, :], w_cat[:, k, cols],
                                     start=True, stop=True).then_inc(folded, 1)

            def router(b):
                if isinstance(b, int):
                    pe.wait_ge(wr_lo_ready, KC)
                else:
                    pe.wait_ge(logits_turned, QUADS * b)
                pe.wait_ge(xT_lo_ready, KC * b + KC)
                for k in range(KC):
                    for xT in (xT_hi, xT_lo):
                        last = nc.tensor.matmul(lT_bank[:, :], wr_hi_lo[:, k, :, :], xT[:, k, :],
                                                start=(k == 0 and xT is xT_hi), stop=(k == KC - 1 and xT is xT_lo))
                last.then_inc(logitsT_done, 1)

            def first_product(b, f):
                if isinstance(b, int) and f in (0, 1, 5):
                    pe.wait_ge(fold_lo_ready, {0: KC + 1, 1: 2 * KC, 5: 3 * KC}[f])
                bank = pre[f % 2]
                cols = slice(f * P, (f + 1) * P)
                if not (isinstance(b, int) and f < 2):
                    pe.wait_ge(h_ready, FT * b + f - 1)
                steps = [(w, xT, k) for w, xTs in ((w1_hi, (xT_hi, xT_lo)), (w1_lo, (xT_hi,)))
                         for k in range(KC) for xT in xTs]
                for n, (w, xT, k) in enumerate(steps):
                    last = nc.tensor.matmul(bank[:, :], w[:, k, cols], xT[:, k, :],
                                            start=(n == 0), stop=(n == len(steps) - 1))
                last.then_inc(pre_done, 1)

            def high(f, j):
                for w in (w2_hi, w2_lo):
                    nc.tensor.matmul(acc[j], h_hi[:, f % SLOTS, j * P:(j + 1) * P], w[:, f, :],
                                     start=(f == 0 and w is w2_hi), stop=False)

            def low(f, j):
                return nc.tensor.matmul(acc[j], h_lo[:, f % SLOTS, j * P:(j + 1) * P], w2_hi[:, f, :],
                                        start=False, stop=(f == FT - 1))

            def second_product(b, f):
                if f == 0 and not isinstance(b, int):
                    pe.wait_ge(y_ready, TT * b)
                pe.wait_ge(h_hi_ready, FT * b + f + 1)
                if f == FT - 1:
                    pe.wait_ge(h_lo_ready, FT * b + f + 1)
                    for j in range(TT):
                        high(f, j)
                        low(f, j).then_inc(tile_done, 1)
                    return
                for j in range(TT):
                    high(f, j)
                pe.wait_ge(h_lo_ready, FT * b + f + 1)
                for j in range(TT):
                    last = low(f, j)
                last.then_inc(acc_done, 1)

            def products(b):
                for f in range(FT):
                    if f == 2 and isinstance(b, int):
                        router(b)
                    first_product(b, f)
                    if f == 0 and not isinstance(b, int):
                        second_product(b - 1, FT - 1)
                    if f >= LAG and f - LAG < FT - TAIL:
                        if isinstance(b, int) and f == LAG:
                            pe.wait_ge(fold_lo_ready, KC * 3)
                            pe.wait_ge(w2_lo_ready, 1)
                        if isinstance(b, int) and f == LAG + FT // 2:
                            pe.wait_ge(w2_lo_ready, 2)
                        second_product(b, f - LAG)

            transpose_first_x()
            fold(0)
            fold(1)
            fold(2)
            products(0)
            with pe.Fori(1, N_BLOCKS) as b:
                for f in range(FT - TAIL, FT - 1):
                    second_product(b - 1, f)
                router(b)
                products(b)
            for f in range(FT - TAIL, FT):
                second_product(N_BLOCKS - 1, f)


def kernel(**inputs):
    import concourse.bacc as _bacc
    from concourse.bass_utils import run_bass_kernel_spmd as _run

    q_right = np.asarray(inputs["L0_cond_q_right"])
    n_quat, lanes = q_right.shape
    n_experts, hidden = inputs["L0_ffn_b1"].shape
    component, sign = rotation_terms()
    by_lane = [np.reshape(a, (-1, lanes // 2, 2)) for a in
               (inputs["cond_256"], q_right, inputs["L0_cond_spectral_gate"])]
    left, right, gate = [a.transpose(1, 2, 0) for a in by_lane]
    quat_rows = np.concatenate([np.concatenate(
        [left[:, :, [0, 1, 1, 1]], right[:, :, component[o].reshape(16)], gate], axis=2) for o in range(n_quat)])
    sign_rows = np.repeat(sign.reshape(n_quat, 16), lanes // 2, axis=0)
    arrays = {
        "x": inputs["x"],
        "quat_rows": np.concatenate([quat_rows.reshape(P, -1), sign_rows], axis=1),
        "router_rows": np.concatenate([inputs["L0_ffn_Wr"],
                                       np.reshape(inputs["L0_ffn_b1"][n_experts - 1], (hidden // P, P))], axis=1),
        "W1": inputs["L0_ffn_W1"],
        "W2": inputs["L0_ffn_W2"],
        "b2": inputs["L0_ffn_b2"],
    }
    arrays = {name: np.ascontiguousarray(a) for name, a in arrays.items()}
    nc = _bacc.Bacc("TRN2", target_bir_lowering=False, num_devices=1)
    args = [nc.dram_tensor(f"in_{name}", a.shape, mybir.dt.from_np(a.dtype), kind="ExternalInput").ap()
            for name, a in arrays.items()]
    out = nc.dram_tensor("out", arrays["x"].shape, F32, kind="ExternalOutput").ap()
    adaln_ffn(nc, *args, out)
    r = _run(nc, [{f"in_{name}": a for name, a in arrays.items()}], core_ids=[0])
    return r.results[0]["out"]
```
